# Optimizing a Trainium2 kernel written in Bass

```python
import numpy as np
import jax
import jax.numpy as jnp

def _softmax(x, axis=-1):
    return jax.nn.softmax(x, axis=axis)

def _gelu(x):
    return jax.nn.gelu(x, approximate=True)

def _silu(x):
    return jax.nn.silu(x)

def _sigmoid(x):
    return jax.nn.sigmoid(x)

def _layernorm(x, axis=-1, eps=1e-05):
    m = jnp.mean(x, axis=axis, keepdims=True)
    v = jnp.var(x, axis=axis, keepdims=True)
    return (x - m) / jnp.sqrt(v + eps)

def _scatter_add(tgt, idx, src, axis=0):
    return tgt.at[idx].add(src)

def _segment_sum(src, seg, n):
    return jax.ops.segment_sum(src, seg, n)
kernel_name = 'mk_seq_preln_d1_jaxref_r8_f87ca2'

def setup_inputs(seed: int=0):
    np.random.seed(seed)
    _w = jnp.asarray

    def _L0_attn_setup():
        import jax, jax.numpy as jnp
        import numpy as np
        N_EMBD = 128
        BLOCK_SIZE = 256
        B = 8
        LN_EPS = 1e-05

        def _mlp(x, W1, b1, W2, b2):
            h = jax.nn.gelu(x @ W1 + b1, approximate=False)
            return h @ W2 + b2
        key = jax.random.key(seed)
        ks = jax.random.split(key, 14)
        C = N_EMBD
        std = 0.02
        d = {'x': jax.random.normal(ks[0], (B, BLOCK_SIZE, C), dtype=jnp.float32)}
        names = ['q', 'k', 'v']
        i = 1
        for n in names:
            d[f'W1{n}'] = jax.random.normal(ks[i], (C, C), dtype=jnp.float32) * std
            i += 1
            d[f'b1{n}'] = jnp.zeros((C,), dtype=jnp.float32)
            d[f'W2{n}'] = jax.random.normal(ks[i], (C, C), dtype=jnp.float32) * std
            i += 1
            d[f'b2{n}'] = jnp.zeros((C,), dtype=jnp.float32)
        d['ln_w'] = jnp.ones((C,), dtype=jnp.float32)
        d['ln_b'] = jnp.zeros((C,), dtype=jnp.float32)
        return d
    _L0_attn_in = _L0_attn_setup()

    def _L0_ffn_setup():
        import jax, jax.numpy as jnp
        import numpy as np
        EPS = 1e-12

        def rms_norm(t, gamma):
            n = jnp.maximum(jnp.linalg.norm(t, axis=-1, keepdims=True), EPS)
            scale = jnp.sqrt(jnp.asarray(t.shape[-1], t.dtype))
            return t / n * scale * gamma
        key = jax.random.key(seed)
        ks = jax.random.split(key, 4)
        b, s, d = (4, 512, 128)
        e, t = (8, 64)
        hidden = 4 * d
        return {'x': jax.random.normal(ks[0], (b, s, d), dtype=jnp.float32), 'gamma_x': jnp.ones((d,), dtype=jnp.float32), 'gamma_slot': jnp.ones((d,), dtype=jnp.float32), 'slot_embeds': jax.random.normal(ks[1], (e, t, d), dtype=jnp.float32), 'w1': jax.random.normal(ks[2], (d, hidden), dtype=jnp.float32) * (1.0 / np.sqrt(d)), 'w2': jax.random.normal(ks[3], (hidden, d), dtype=jnp.float32) * (1.0 / np.sqrt(hidden))}
    _L0_ffn_in = _L0_ffn_setup()
    _d = {'L0_attn_x': _L0_attn_in['x'], 'L0_attn_W1q': _L0_attn_in['W1q'], 'L0_attn_b1q': _L0_attn_in['b1q'], 'L0_attn_W2q': _L0_attn_in['W2q'], 'L0_attn_b2q': _L0_attn_in['b2q'], 'L0_attn_W1k': _L0_attn_in['W1k'], 'L0_attn_b1k': _L0_attn_in['b1k'], 'L0_attn_W2k': _L0_attn_in['W2k'], 'L0_attn_b2k': _L0_attn_in['b2k'], 'L0_attn_W1v': _L0_attn_in['W1v'], 'L0_attn_b1v': _L0_attn_in['b1v'], 'L0_attn_W2v': _L0_attn_in['W2v'], 'L0_attn_b2v': _L0_attn_in['b2v'], 'L0_attn_ln_w': _L0_attn_in['ln_w'], 'L0_attn_ln_b': _L0_attn_in['ln_b'], 'L0_ffn_gamma_x': _L0_ffn_in['gamma_x'], 'L0_ffn_gamma_slot': _L0_ffn_in['gamma_slot'], 'L0_ffn_slot_embeds': _L0_ffn_in['slot_embeds'], 'L0_ffn_w1': _L0_ffn_in['w1'], 'L0_ffn_w2': _L0_ffn_in['w2']}
    _x0 = _d['L0_attn_x']
    _d['L0_attn_x'] = jax.random.normal(jax.random.fold_in(jax.random.key(seed), 1), (8, 256, 128), dtype=_x0.dtype)
    del _x0
    return _d

def reference(L0_attn_x, L0_attn_W1q, L0_attn_b1q, L0_attn_W2q, L0_attn_b2q, L0_attn_W1k, L0_attn_b1k, L0_attn_W2k, L0_attn_b2k, L0_attn_W1v, L0_attn_b1v, L0_attn_W2v, L0_attn_b2v, L0_attn_ln_w, L0_attn_ln_b, L0_ffn_gamma_x, L0_ffn_gamma_slot, L0_ffn_slot_embeds, L0_ffn_w1, L0_ffn_w2):

    def _L0_attn_ref(x, W1q, b1q, W2q, b2q, W1k, b1k, W2k, b2k, W1v, b1v, W2v, b2v, ln_w, ln_b):
        import jax, jax.numpy as jnp
        import numpy as np
        N_EMBD = 128
        BLOCK_SIZE = 256
        B = 8
        LN_EPS = 1e-05

        def _mlp(x, W1, b1, W2, b2):
            h = jax.nn.gelu(x @ W1 + b1, approximate=False)
            return h @ W2 + b2
        Bsz, T, C = x.shape
        q = _mlp(x, W1q, b1q, W2q, b2q)
        k = _mlp(x, W1k, b1k, W2k, b2k)
        v = _mlp(x, W1v, b1v, W2v, b2v)
        scale = np.sqrt(N_EMBD * BLOCK_SIZE).astype(np.float32)
        scores = jnp.einsum('bid,bjd->bij', q, k) / scale
        mask = jnp.tril(jnp.ones((T, T), dtype=scores.dtype))
        scores = scores * mask
        out = jnp.einsum('bij,bjd->bid', scores, v)
        mu = jnp.mean(out, axis=-1, keepdims=True)
        var = jnp.mean(jnp.square(out - mu), axis=-1, keepdims=True)
        out = (out - mu) * jax.lax.rsqrt(var + LN_EPS) * ln_w + ln_b
        return out

    def _L0_ffn_ref(x, gamma_x, gamma_slot, slot_embeds, w1, w2):
        import jax, jax.numpy as jnp
        import numpy as np
        EPS = 1e-12

        def rms_norm(t, gamma):
            n = jnp.maximum(jnp.linalg.norm(t, axis=-1, keepdims=True), EPS)
            scale = jnp.sqrt(jnp.asarray(t.shape[-1], t.dtype))
            return t / n * scale * gamma
        b, s, d = x.shape
        e, t, _ = slot_embeds.shape
        xn = rms_norm(x, gamma_x)
        se = rms_norm(slot_embeds, gamma_slot)
        logits = jnp.einsum('bsd,etd->bset', xn, se)
        dispatch = jax.nn.softmax(logits, axis=1)
        slots = jnp.einsum('bsd,bset->betd', xn, dispatch)
        h = jax.nn.gelu(slots @ w1, approximate=False)
        processed = h @ w2
        combine = jax.nn.softmax(logits.reshape(b, s, e * t), axis=-1)
        out = jnp.einsum('bnd,bsn->bsd', processed.reshape(b, e * t, d), combine)
        return out
    x = L0_attn_x
    x = x + _L0_attn_ref(_layernorm(x, axis=-1), L0_attn_W1q, L0_attn_b1q, L0_attn_W2q, L0_attn_b2q, L0_attn_W1k, L0_attn_b1k, L0_attn_W2k, L0_attn_b2k, L0_attn_W1v, L0_attn_b1v, L0_attn_W2v, L0_attn_b2v, L0_attn_ln_w, L0_attn_ln_b)
    x = x + _L0_ffn_ref(_layernorm(x, axis=-1), L0_ffn_gamma_x, L0_ffn_gamma_slot, L0_ffn_slot_embeds, L0_ffn_w1, L0_ffn_w2)
    return x

_drawn_inputs = setup_inputs


def setup_inputs(seed=0):
    import zlib

    import numpy as np

    out = dict(_drawn_inputs(seed))
    spreads = {'L0_attn_b1q': (0.0, 0.1),
     'L0_attn_b2q': (0.0, 0.1),
     'L0_attn_b1k': (0.0, 0.1),
     'L0_attn_b2k': (0.0, 0.1),
     'L0_attn_b1v': (0.0, 0.1),
     'L0_attn_b2v': (0.0, 0.1),
     'L0_attn_ln_w': (1.0, 0.2),
     'L0_attn_ln_b': (0.0, 0.1),
     'L0_ffn_gamma_x': (1.0, 0.2),
     'L0_ffn_gamma_slot': (1.0, 0.2)}
    factors = {}
    for name, (base, spread) in spreads.items():
        noise = np.random.default_rng([zlib.crc32(name.encode()), seed]).standard_normal(out[name].shape)
        drawn = base * np.exp(spread * noise) if base else spread * noise
        out[name] = jnp.asarray(drawn.astype(out[name].dtype))
    for name, factor in factors.items():
        out[name] = (out[name] * factor).astype(out[name].dtype)
    return out
```

```python
from contextlib import ExitStack

import concourse.bass as bass
from concourse import mybir

F32 = mybir.dt.float32
F32R = mybir.dt.float32r
ALU = mybir.AluOpType
ACT = mybir.ActivationFunctionType
AX = mybir.AxisListType

LN_EPS = 1e-5
RMS_EPS = 1e-12
HI, LO = 0, 1
ATTN, ROUTE, EXPERT = range(3)


def build(nc, x, W1q, b1q, W2q, b2q, W1k, b1k, W2k, b2k, W1v, b1v, W2v, b2v, ln_w, ln_b,
          gamma_x, gamma_slot, slot_embeds, w1, w2, out):
    B, T, C = x.shape
    P = 128
    NT = T // P
    E = slot_embeds.shape[0] * slot_embeds.shape[1]
    NE = E // P
    HID = w1.shape[1]
    NH = HID // P
    NG = 2
    GH = NH // NG
    assert C == P and NT == 2 and NE == 4 and NH == 4
    inv_scale = 1.0 / float((C * T) ** 0.5)
    SW = T + P
    X_GROUPS = [(0, 1), (1, 3), (3, B)]

    x_v = x.rearrange("b (t p) c -> p b t c", p=P)
    out_v = out.rearrange("b (t p) c -> p b t c", p=P)

    ctx = ExitStack()
    with ctx:
        def sb(name, shape, dt=F32):
            return ctx.enter_context(nc.sbuf_tensor(name, [P] + list(shape), dt))

        def sem(name):
            return ctx.enter_context(nc.semaphore(name))

        x_sb = sb("x_sb", [B, NT, C])
        W1_raw = sb("W1_raw", [3, C])
        W1_s = sb("W1_s", [3, 2, C], F32R)
        W2_sb = sb("W2_sb", [3, C])
        b1_col = sb("b1_col", [3])
        b2_col = sb("b2_col", [2])
        b2v_row = sb("b2v_row", [C])
        lnw_row = sb("lnw_row", [C])
        lnb_row = sb("lnb_row", [C])
        gx_col = sb("gx_col", [1])
        gs_col = sb("gs_col", [1])
        gg_col = sb("gg_col", [1])
        slot_raw = sb("slot_raw", [NE, C])
        slot_sq = sb("slot_sq", [NE, C])
        slot_n = sb("slot_n", [NE, C])
        slot_ss = sb("slot_ss", [NE])
        slot_ms = sb("slot_ms", [NE])
        slot_r = sb("slot_r", [NE])
        slotT_s = sb("slotT_s", [2, E], F32R)
        w1_raw = sb("w1_raw", [HID])
        w1_s = sb("w1_s", [2, HID], F32R)
        w2_raw = sb("w2_raw", [NH, C])
        w2_s = sb("w2_s", [2, NH, C], F32R)
        ident = sb("ident", [P])
        mask = sb("mask", [SW])
        minus_half = sb("minus_half", [B * NT])
        gelu_warm = sb("gelu_warm", [1])

        x_bst = sb("x_bst", [B, NT, 6])
        x_mv = sb("x_mv", [B, NT, 2])
        x_ve = sb("x_ve", [B * NT])
        x_rs = sb("x_rs", [B * NT])
        x_nb = sb("x_nb", [B * NT])
        xn = sb("xn", [NT, C])
        xT_s = sb("xT_s", [2, T], F32R)
        hidT = sb("hidT", [3, T])
        qkT = sb("qkT", [2, T])
        v_sb = sb("v_sb", [NT, C])
        sT = sb("sT", [SW])
        a_bst = sb("a_bst", [NT, 6])
        a_mv = sb("a_mv", [NT, 2])
        a_ve = sb("a_ve", [NT])
        a_rs = sb("a_rs", [NT])
        ac = sb("ac", [NT, C])
        xb = sb("xb", [NT, C])
        x1_cur = sb("x1_cur", [NT, C])
        z_bst = sb("z_bst", [NT, 6])
        z_mv = sb("z_mv", [NT, 2])
        z_nm = sb("z_nm", [NT])
        z_u = sb("z_u", [NT])
        z_w = sb("z_w", [NT])
        z_rs = sb("z_rs", [NT])
        z_cur = sb("z_cur", [NT, C])

        x1_all = sb("x1_all", [B, NT, C])
        z_all = sb("z_all", [B, NT, C])
        zT_all = sb("zT_all", [B, 2, T], F32R)
        slots_all = sb("slots_all", [B, 2, E], F32R)
        CT_all = sb("CT_all", [B, NE, T])
        ZC_all = sb("ZC_all", [B, NT])
        rZC_all = sb("rZC_all", [B, NT])

        z_st = sb("z_st", [NT, C])
        zT_st = sb("zT_st", [2, T], F32R)
        nmC = sb("nmC", [NT])
        nmD = sb("nmD", [NE])
        ZD = sb("ZD", [NE])
        rZD = sb("rZD", [NE])
        Cx = sb("Cx", [NT, E])
        Dx = sb("Dx", [NE, T])
        Dn = sb("Dn", [NE, T])
        D_sb = sb("D_sb", [NT, E])

        CT_st = sb("CT_st", [NE, T])
        h_f = sb("h_f", [NG, GH, E])
        h_hi = sb("h_hi", [NG, GH, E], F32R)
        h_lo = sb("h_lo", [NG, GH, E], F32R)
        PT_sb = sb("PT_sb", [E])
        P_sb = sb("P_sb", [NE, C])
        out_sb = sb("out_sb", [NT, C])

        ps = ctx.enter_context(nc.psum_tensor("ps", [P, 8, 512], F32))
        xT_ps = ps[:, 0, 0:T]
        hqk_ps = ps[:, 1, :].rearrange("p (m t) -> p m t", m=2)
        hv_ps = ps[:, 2, 0:T]
        qk_ps = ps[:, 3, :].rearrange("p (m t) -> p m t", m=2)
        v_ps = ps[:, 4, 0:NT * C].rearrange("p (t c) -> p t c", t=NT)
        s_ps = ps[:, 5, 0:SW]
        a_ps = ps[:, 6, 0:NT * C].rearrange("p (t c) -> p t c", t=NT)
        zT_ps = ps[:, 7, 0:T]
        slotT_ps = ps[:, 7, :]
        L_ps = ps[:, 1:3, :]
        LT_ps = ps[:, 3:5, :].rearrange("p k (e t) -> p (k e) t", e=2)
        D_ps = ps[:, 5:7, :]
        CT_ps = ps[:, 5:7, :].rearrange("p k (e t) -> p (k e) t", e=2)
        slots_ps = ps[:, 0, :]
        h_ps = [ps[:, 1:3, :], ps[:, 3:5, :]]
        PT_ps = ps[:, 7, :]
        P_ps = ps[:, 5, :].rearrange("p (e c) -> p e c", e=NE)
        out_ps = ps[:, 6, 0:NT * C].rearrange("p (t c) -> p t c", t=NT)

        ld_x = [sem(f"ld_x{g}") for g in range(len(X_GROUPS))]
        ld_W1, ld_W2, ld_b, ld_rows, ld_slot, ld_w = (
            sem("ld_W1"), sem("ld_W2"), sem("ld_b"), sem("ld_rows"), sem("ld_slot"), sem("ld_w"))
        ident_set, mask_set, half_set, gelu_warmed = (
            sem("ident_set"), sem("mask_set"), sem("half_set"), sem("gelu_warmed"))
        W1_split, w_split, gg_set = sem("W1_split"), sem("w_split"), sem("gg_set")
        slot_sq_done, slot_ms_set, slot_r_set, slot_n_set = (
            sem("slot_sq_done"), sem("slot_ms_set"), sem("slot_r_set"), sem("slot_n_set"))
        slot_turned, slotT_hi, slotT_lo = sem("slot_turned"), sem("slotT_hi"), sem("slotT_lo")

        x_stats, x_moments, x_eps, x_rstd, x_nb_set = (
            sem("x_stats"), sem("x_moments"), sem("x_eps"), sem("x_rstd"), sem("x_nb_set"))
        xn_ready, x_turned, xT_hi, xT_lo = sem("xn_ready"), sem("x_turned"), sem("xT_hi"), sem("xT_lo")
        hid_mm, hid_ready = sem("hid_mm"), sem("hid_ready")
        qk_mm, qk_ready, v_mm, v_ready = sem("qk_mm"), sem("qk_ready"), sem("v_mm"), sem("v_ready")
        s_mm, s_ready, a_mm = sem("s_mm"), sem("s_ready"), sem("a_mm")
        a_stats, a_moments, a_eps, a_rstd, ac_ready = (
            sem("a_stats"), sem("a_moments"), sem("a_eps"), sem("a_rstd"), sem("ac_ready"))
        xb_ready, x1_ready = sem("xb_ready"), sem("x1_ready")
        z_stats, z_moments, z_u_set, z_w_set, z_rstd, z_ready = (
            sem("z_stats"), sem("z_moments"), sem("z_u_set"), sem("z_w_set"), sem("z_rstd"), sem("z_ready"))
        x1_saved, z_saved = sem("x1_saved"), sem("z_saved")
        z_turned, zT_hi, zT_lo = sem("z_turned"), sem("zT_hi"), sem("zT_lo")

        z_staged, zT_staged = sem("z_staged"), sem("zT_staged")
        LT_mm, L_mm, D_max, C_max = sem("LT_mm"), sem("L_mm"), sem("D_max"), sem("C_max")
        D_exp, C_exp, ZD_inv, ZC_inv, Dn_ready = (
            sem("D_exp"), sem("C_exp"), sem("ZD_inv"), sem("ZC_inv"), sem("Dn_ready"))
        D_turned, D_ready, C_turned, CT_ready = sem("D_turned"), sem("D_ready"), sem("C_turned"), sem("CT_ready")
        slots_mm, slots_hi, slots_lo = sem("slots_mm"), sem("slots_hi"), sem("slots_lo")

        CT_staged = sem("CT_staged")
        h_mm, h_ready, h_hi_ready, h_lo_ready, PT_mm = (
            sem("h_mm"), sem("h_ready"), sem("h_hi_ready"), sem("h_lo_ready"), sem("PT_mm"))
        PT_ready, P_turned, P_ready, out_mm, out_ready = (
            sem("PT_ready"), sem("P_turned"), sem("P_ready"), sem("out_mm"), sem("out_ready"))
        out_stored = sem("out_stored")

        block = ctx.enter_context(nc.Block())

        SCHEDULE = [(ATTN, -1, 3), (ATTN, 3, B - 1), (ATTN, B - 1, B + 1), (ROUTE, -1, 0), (ATTN, B + 1, B + 2),
                    (ROUTE, 0, 1), (ROUTE, 1, B - 1), (ROUTE, B - 1, B), (EXPERT, -1, 2), (EXPERT, 2, B - 1),
                    (EXPERT, B - 1, B + 1)]
        LOOPS = [(ATTN, 3, B - 1), (ROUTE, 1, B - 1), (EXPERT, 2, B - 1)]

        def run(eng, phases, before):
            for part in SCHEDULE:
                phase, k0, k1 = part
                stages = phases[phase]
                if part in LOOPS:
                    before.get((phase, k0), lambda: None)()
                    if not stages:
                        continue
                    offsets = [o for o, _ in stages]
                    with eng.Fori(k0, k1) as k:
                        at = {o: in_register(eng, k + o, k1 - 1 + o) for o in range(min(offsets), max(offsets) + 2)}
                        for o, stage in stages:
                            stage(at[o], at[o + 1])
                else:
                    for k in range(k0, k1):
                        before.get((phase, k), lambda: None)()
                        for o, stage in stages:
                            if 0 <= k + o < B:
                                stage(k + o, k + o + 1)

        def in_register(eng, value, most):
            return eng.snap(eng.to_reg(value), min_val=0, max_val=most)

        def freed(eng, semaphore, count):
            if not (isinstance(count, int) and count <= 0):
                eng.wait_ge(semaphore, count)

        def own_instruction(eng):
            eng.wait_ge(half_set, 1)

        @block.sync
        def _(sp):
            sp.dma_start(x_sb[:, 0], x_v[:, 0]).then_inc(ld_x[0], 16)
            for m, W in enumerate((W1q, W1k, W1v)):
                sp.dma_start(W1_raw[:, m], W).then_inc(ld_W1, 16)
            for m, b in enumerate((b1q, b1k, b1v)):
                sp.dma_start(b1_col[:, m:m + 1], b[:, None]).then_inc(ld_b, 16)
            sp.dma_start(x_sb[:, 1:3], x_v[:, 1:3]).then_inc(ld_x[1], 16)
            for m, W in enumerate((W2q, W2k, W2v)):
                sp.dma_start(W2_sb[:, m], W).then_inc(ld_W2, 16)
            for m, b in enumerate((b2q, b2k)):
                sp.dma_start(b2_col[:, m:m + 1], b[:, None]).then_inc(ld_b, 16)
            sp.dma_start(x_sb[:, 3:B], x_v[:, 3:B]).then_inc(ld_x[2], 16)

            def save_x1(b, n):
                own_instruction(sp)
                sp.wait_ge(x1_ready, n)
                sp.dma_start(x1_all[:, b], x1_cur[:, :, :]).then_inc(x1_saved, 16)

            def save_z(b, n):
                own_instruction(sp)
                sp.wait_ge(z_ready, n)
                sp.dma_start(z_all[:, b], z_cur[:, :, :]).then_inc(z_saved, 16)

            def stage_zT(b, n):
                own_instruction(sp)
                sp.wait_ge(zT_hi, n)
                sp.wait_ge(zT_lo, n)
                freed(sp, L_mm, b)
                sp.dma_start(zT_st[:, :, :].bitcast(F32), zT_all[:, b].bitcast(F32)).then_inc(zT_staged, 16)

            def stage_z(b, n):
                landed = 16 * n if isinstance(n, int) else in_register(sp, 16 * n, 16 * B)
                own_instruction(sp)
                sp.wait_ge(z_saved, landed)
                freed(sp, slots_mm, b)
                sp.dma_start(z_st[:, :, :], z_all[:, b]).then_inc(z_staged, 16)

            def stage_CT(b, n):
                own_instruction(sp)
                sp.wait_ge(CT_ready, n)
                freed(sp, out_mm, b)
                sp.dma_start(CT_st[:, :, :], CT_all[:, b]).then_inc(CT_staged, 16)

            def store(b, n):
                own_instruction(sp)
                sp.wait_ge(out_ready, n)
                sp.dma_start(out_v[:, b], out_sb[:, :, :]).then_inc(out_stored, 16)

            run(sp, [[(-2, save_z), (-1, save_x1)], [(1, stage_zT), (0, stage_z)], [(0, stage_CT), (-1, store)]], {})
            sp.wait_ge(out_stored, 16 * B)

        @block.gpsimd
        def _(pool):
            nc.gpsimd.memset(minus_half[:, :], -0.5).then_inc(half_set, 1)
            nc.gpsimd.memset(ident[:, :], 0.0).then_inc(ident_set, 1)
            nc.gpsimd.memset(mask[:, :], inv_scale).then_inc(mask_set, 1)
            pool.wait_ge(ident_set, 1)
            nc.gpsimd.affine_select(out=ident[:, :], in_=ident[:, :], compare_op=ALU.not_equal, fill=1.0,
                                    base=0, pattern=[[-1, P]], channel_multiplier=1).then_inc(ident_set, 1)
            for row, b in ((b2v_row, b2v), (lnw_row, ln_w), (lnb_row, ln_b)):
                pool.dma_start(row[:, :], b.partition_broadcast(P)).then_inc(ld_rows, 16)
            pool.dma_start(slot_raw[:, :, :],
                           slot_embeds.rearrange("e t c -> (e t) c").rearrange("(k p) c -> p k c", p=P)
                           ).then_inc(ld_slot, 16)
            pool.dma_start(gx_col[:, :], gamma_x[:, None]).then_inc(ld_slot, 16)
            pool.dma_start(gs_col[:, :], gamma_slot[:, None]).then_inc(ld_slot, 16)
            pool.dma_start(w1_raw[:, :], w1).then_inc(ld_w, 16)
            pool.dma_start(w2_raw[:, :, :], w2.rearrange("(k p) c -> p k c", p=P)).then_inc(ld_w, 16)

            def mask_triangles():
                pool.wait_ge(mask_set, 1)
                for c0 in (0, T):
                    tri = mask[:, c0:c0 + P]
                    nc.gpsimd.affine_select(out=tri, in_=tri, compare_op=ALU.is_ge, fill=0.0, base=0,
                                            pattern=[[1, P]], channel_multiplier=-1).then_inc(mask_set, 1)

            def x_rsqrt(g):
                b0, b1 = X_GROUPS[g]
                cols = slice(b0 * NT, b1 * NT)
                pool.wait_ge(half_set, 1)
                pool.wait_ge(x_moments, g + 1)
                nc.gpsimd.tensor_scalar(x_ve[:, cols], x_mv[:, b0:b1, :, 1].rearrange("p b t -> p (b t)"),
                                        LN_EPS, 1.0, ALU.add, ALU.mult).then_inc(x_eps, 1)
                pool.wait_ge(x_eps, g + 1)
                nc.gpsimd.tensor_tensor(x_rs[:, cols], x_ve[:, cols], minus_half[:, 0:(b1 - b0) * NT], ALU.pow
                                        ).then_inc(x_rstd, 1)

            def slot_rsqrt():
                pool.wait_ge(slot_ms_set, 1)
                nc.gpsimd.tensor_tensor(slot_r[:, :], slot_ms[:, :], minus_half[:, 0:NE], ALU.pow
                                        ).then_inc(slot_r_set, 1)

            def split_w1():
                pool.wait_ge(ld_w, 32)
                nc.gpsimd.tensor_copy(w1_s[:, HI], w1_raw[:, :]).then_inc(w_split, 1)
                pool.wait_ge(w_split, 1)
                nc.gpsimd.tensor_tensor(w1_s[:, LO], w1_raw[:, :], w1_s[:, HI].bitcast(F32), ALU.subtract
                                        ).then_inc(w_split, 1)

            def split_w2():
                nc.gpsimd.tensor_copy(w2_s[:, HI], w2_raw[:, :, :]).then_inc(w_split, 1)
                pool.wait_ge(w_split, 3)
                nc.gpsimd.tensor_tensor(w2_s[:, LO], w2_raw[:, :, :], w2_s[:, HI].bitcast(F32), ALU.subtract
                                        ).then_inc(w_split, 1)

            def x_plus_bias(b, n):
                freed(pool, x1_ready, b)
                nc.gpsimd.tensor_tensor(xb[:, :, :], x_sb[:, b],
                                        lnb_row[:, :].unsqueeze(1).to_broadcast([P, NT, C]), ALU.add
                                        ).then_inc(xb_ready, 1)

            def a_rsqrt(b, n):
                own_instruction(pool)
                pool.wait_ge(a_moments, n)
                nc.gpsimd.tensor_scalar(a_ve[:, :], a_mv[:, :, 1], LN_EPS, 1.0, ALU.add, ALU.mult
                                        ).then_inc(a_eps, 1)
                pool.wait_ge(a_eps, n)
                freed(pool, x1_ready, b)
                nc.gpsimd.tensor_tensor(a_rs[:, :], a_ve[:, :], minus_half[:, 0:NT], ALU.pow).then_inc(a_rstd, 1)

            def z_rsqrt(b, n):
                pool.wait_ge(z_w_set, n)
                nc.gpsimd.tensor_tensor(z_rs[:, :], z_w[:, :], minus_half[:, 0:NT], ALU.pow).then_inc(z_rstd, 1)

            def z_normalise(b, n):
                landed = 16 * b if isinstance(b, int) else in_register(pool, 16 * b, 16 * B)
                own_instruction(pool)
                pool.wait_ge(z_rstd, n)
                freed(pool, z_turned, b)
                freed(pool, z_saved, landed)
                for t in range(NT):
                    last = nc.gpsimd.tensor_scalar(z_cur[:, t], x1_cur[:, t], z_nm[:, t:t + 1], z_rs[:, t:t + 1],
                                                   ALU.add, ALU.mult)
                last.then_inc(z_ready, 1)

            def D_normalise(b, n):
                own_instruction(pool)
                pool.wait_ge(ZD_inv, n)
                freed(pool, D_turned, b)
                for e in range(NE):
                    last = nc.gpsimd.tensor_scalar(Dn[:, e], Dx[:, e], rZD[:, e:e + 1], 1.0, ALU.mult, ALU.mult)
                last.then_inc(Dn_ready, 1)

            def before_0():
                x_rsqrt(1)
                mask_triangles()
                pool.wait_ge(ld_rows, 48)

            def before_1():
                x_rsqrt(2)
                slot_rsqrt()

            run(pool, [[(-1, x_plus_bias), (-2, z_rsqrt), (-2, z_normalise), (-1, a_rsqrt)],
                       [(1, D_normalise)], []],
                {(ATTN, -1): lambda: x_rsqrt(0), (ATTN, 0): before_0, (ATTN, 1): before_1, (ATTN, 3): split_w1,
                 (ATTN, B - 1): split_w2})

        @block.scalar
        def _(act):
            act.wait_ge(half_set, 1)
            nc.scalar.activation(gelu_warm[:, :], minus_half[:, 0:1], ACT.Gelu).then_inc(gelu_warmed, 1)

            def x_group(g):
                act.wait_ge(ld_x[g], 16)
                act.wait_ge(x_rstd, g + 1)
                act.wait_ge(x_nb_set, g + 1)

            def x_normalise(b, n):
                freed(act, x_turned, b)
                for t in range(NT):
                    last = nc.scalar.activation(xn[:, t], x_sb[:, b, t], ACT.Identity,
                                                bias=x_nb[:, bass.ds(b * NT + t, 1)],
                                                scale=x_rs[:, bass.ds(b * NT + t, 1)])
                last.then_inc(xn_ready, 1)

            def hidden_qk(b, n):
                freed(act, v_mm, b)
                act.wait_ge(hid_mm, 2 * b + 1)
                for m in range(2):
                    nc.scalar.activation(hidT[:, m], hqk_ps[:, m], ACT.Gelu, bias=b1_col[:, m:m + 1]
                                         ).then_inc(hid_ready, 1)

            def hidden_v(b, n):
                act.wait_ge(hid_mm, 2 * b + 2)
                nc.scalar.activation(hidT[:, 2], hv_ps, ACT.Gelu, bias=b1_col[:, 2:3]).then_inc(hid_ready, 1)

            def xT_round(b, n):
                act.wait_ge(x_turned, n)
                freed(act, hid_mm, 2 * b)
                nc.scalar.copy(xT_s[:, HI], xT_ps).then_inc(xT_hi, 1)

            def qk(b, n):
                act.wait_ge(qk_mm, n)
                freed(act, s_mm, b)
                for m in range(2):
                    nc.scalar.activation(qkT[:, m], qk_ps[:, m], ACT.Identity, bias=b2_col[:, m:m + 1]
                                         ).then_inc(qk_ready, 1)

            def zT_round(b, n):
                act.wait_ge(z_turned, n)
                nc.scalar.copy(zT_all[:, b, HI], zT_ps).then_inc(zT_hi, 1)

            def slot_squares():
                act.wait_ge(ld_slot, 48)
                for e in range(NE):
                    nc.scalar.activation(slot_sq[:, e], slot_raw[:, e], ACT.Square,
                                         accum_out=slot_ss[:, e:e + 1]).then_inc(slot_sq_done, 1)

            def slot_round():
                act.wait_ge(slot_turned, 1)
                act.wait_ge(gg_set, 1)
                nc.scalar.activation(slotT_s[:, HI], slotT_ps, ACT.Identity, scale=gg_col[:, 0:1]
                                     ).then_inc(slotT_hi, 1)

            def D_back(b, n):
                act.wait_ge(D_turned, n)
                freed(act, slots_mm, b)
                nc.scalar.copy(D_sb[:, :, :], D_ps).then_inc(D_ready, 1)

            def exp_D(b, n):
                act.wait_ge(D_max, n)
                freed(act, Dn_ready, b)
                freed(act, ZD_inv, b)
                for e in range(NE):
                    last = nc.scalar.activation(Dx[:, e], LT_ps[:, e], ACT.Exp, bias=nmD[:, e:e + 1],
                                                accum_out=ZD[:, e:e + 1])
                last.then_inc(D_exp, 1)

            def slots_round(b, n):
                act.wait_ge(slots_mm, n)
                nc.scalar.activation(slots_all[:, b, HI], slots_ps, ACT.Identity, scale=gx_col[:, 0:1]
                                     ).then_inc(slots_hi, 1)

            def exp_C(b, n):
                act.wait_ge(C_max, n)
                freed(act, C_turned, b)
                for t in range(NT):
                    last = nc.scalar.activation(Cx[:, t], L_ps[:, t], ACT.Exp, bias=nmC[:, t:t + 1],
                                                accum_out=ZC_all[:, b, t:t + 1])
                last.then_inc(C_exp, 1)

            def gelu_group(g):
                def stage(b, n):
                    act.wait_ge(h_mm, NG * b + g + 1)
                    freed(act, h_lo_ready, NG * b + g - 1)
                    nc.scalar.activation(h_f[:, g], h_ps[g], ACT.Gelu).then_inc(h_ready, 1)
                    act.wait_ge(h_ready, NG * b + g + 1)
                    freed(act, PT_mm, NG * b + g - 1)
                    nc.scalar.copy(h_hi[:, g], h_f[:, g]).then_inc(h_hi_ready, 1)
                return stage

            def P_copy(b, n):
                act.wait_ge(P_turned, n)
                freed(act, out_mm, b)
                nc.scalar.copy(P_sb[:, :, :], P_ps).then_inc(P_ready, 1)

            def before_0():
                x_group(1)
                act.wait_ge(ld_b, 80)

            def before_1():
                slot_squares()
                slot_round()

            run(act, [[(1, x_normalise), (0, hidden_qk), (0, hidden_v), (1, xT_round), (0, qk), (-2, zT_round)],
                      [(0, D_back), (1, exp_D), (0, slots_round), (1, exp_C)],
                      [(1, gelu_group(0)), (1, gelu_group(1)), (0, P_copy)]],
                {(ATTN, -1): lambda: x_group(0), (ATTN, 0): before_0, (ATTN, 1): before_1,
                 (ATTN, 2): lambda: x_group(2)})

        @block.vector
        def _(dve):
            def x_moments_of(g):
                b0, b1 = X_GROUPS[g]
                dve.wait_ge(ld_x[g], 16)
                for b in range(b0, b1):
                    for t in range(NT):
                        last = nc.vector.bn_stats(x_bst[:, b, t], x_sb[:, b, t])
                last.then_inc(x_stats, 1)
                dve.wait_ge(x_stats, g + 1)
                for b in range(b0, b1):
                    for t in range(NT):
                        last = nc.vector.bn_aggr(x_mv[:, b, t], x_bst[:, b, t])
                last.then_inc(x_moments, 1)

            def x_bias(g):
                b0, b1 = X_GROUPS[g]
                cols = slice(b0 * NT, b1 * NT)
                dve.wait_ge(x_moments, g + 1)
                dve.wait_ge(x_rstd, g + 1)
                nc.vector.scalar_tensor_tensor(out=x_nb[:, cols],
                                               in0=x_mv[:, b0:b1, :, 0].rearrange("p b t -> p (b t)"), scalar=-1.0,
                                               in1=x_rs[:, cols], op0=ALU.mult, op1=ALU.mult).then_inc(x_nb_set, 1)

            def split_W1():
                dve.wait_ge(ld_W1, 48)
                nc.vector.tensor_copy(W1_s[:, :, HI], W1_raw[:, :, :]).then_inc(W1_split, 1)
                dve.wait_ge(W1_split, 1)
                nc.vector.tensor_tensor(W1_s[:, :, LO], W1_raw[:, :, :], W1_s[:, :, HI].bitcast(F32),
                                        ALU.subtract).then_inc(W1_split, 1)

            def slot_mean_square():
                dve.wait_ge(slot_sq_done, NE)
                nc.vector.tensor_scalar(slot_ms[:, :], slot_ss[:, :], 1.0 / C, RMS_EPS ** 2 / C,
                                        ALU.mult, ALU.max).then_inc(slot_ms_set, 1)
                dve.wait_ge(ld_slot, 48)
                nc.vector.tensor_tensor(gg_col[:, :], gx_col[:, :], gs_col[:, :], ALU.mult).then_inc(gg_set, 1)

            def slot_normalise():
                dve.wait_ge(slot_r_set, 1)
                for e in range(NE):
                    last = nc.vector.tensor_scalar(slot_n[:, e], slot_raw[:, e], slot_r[:, e:e + 1], None, ALU.mult)
                last.then_inc(slot_n_set, 1)

            def slot_rest():
                dve.wait_ge(slotT_hi, 1)
                nc.vector.scalar_tensor_tensor(out=slotT_s[:, LO], in0=slotT_ps, scalar=gg_col[:, 0:1],
                                               in1=slotT_s[:, HI].bitcast(F32), op0=ALU.mult, op1=ALU.subtract
                                               ).then_inc(slotT_lo, 1)

            def xT_rest(b, n):
                dve.wait_ge(xT_hi, n)
                freed(dve, hid_mm, 2 * b)
                nc.vector.tensor_tensor(xT_s[:, LO], xT_ps, xT_s[:, HI].bitcast(F32), ALU.subtract
                                        ).then_inc(xT_lo, 1)

            def v_bias(b, n):
                dve.wait_ge(v_mm, n)
                freed(dve, a_mm, b)
                nc.vector.tensor_tensor(v_sb[:, :, :], v_ps,
                                        b2v_row[:, :].unsqueeze(1).to_broadcast([P, NT, C]), ALU.add
                                        ).then_inc(v_ready, 1)

            def mask_scores(b, n):
                dve.wait_ge(s_mm, n)
                freed(dve, a_mm, b)
                nc.vector.tensor_tensor(sT[:, :], s_ps, mask[:, :], ALU.mult).then_inc(s_ready, 1)

            def a_sums(b, n):
                dve.wait_ge(a_mm, n)
                for t in range(NT):
                    last = nc.vector.bn_stats(a_bst[:, t], a_ps[:, t])
                last.then_inc(a_stats, 1)

            def a_centre(b, n):
                own_instruction(dve)
                dve.wait_ge(a_stats, n)
                freed(dve, a_rstd, b)
                for t in range(NT):
                    last = nc.vector.bn_aggr(a_mv[:, t], a_bst[:, t])
                last.then_inc(a_moments, 1)
                dve.wait_ge(a_moments, n)
                freed(dve, x1_ready, b)
                for t in range(NT):
                    last = nc.vector.scalar_tensor_tensor(out=ac[:, t], in0=a_ps[:, t], scalar=a_mv[:, t, 0:1],
                                                          in1=lnw_row[:, :], op0=ALU.subtract, op1=ALU.mult)
                last.then_inc(ac_ready, 1)

            def residual(b, n):
                dve.wait_ge(a_rstd, n)
                dve.wait_ge(ac_ready, n)
                dve.wait_ge(xb_ready, n)
                freed(dve, z_ready, b)
                freed(dve, x1_saved, 16 * b)
                for t in range(NT):
                    last = nc.vector.scalar_tensor_tensor(out=x1_cur[:, t], in0=ac[:, t], scalar=a_rs[:, t:t + 1],
                                                          in1=xb[:, t], op0=ALU.mult, op1=ALU.add)
                last.then_inc(x1_ready, 1)

            def z_sums(b, n):
                dve.wait_ge(x1_ready, n)
                for t in range(NT):
                    last = nc.vector.bn_stats(z_bst[:, t], x1_cur[:, t])
                last.then_inc(z_stats, 1)

            def z_variance(b, n):
                own_instruction(dve)
                dve.wait_ge(z_stats, n)
                freed(dve, z_ready, b)
                for t in range(NT):
                    last = nc.vector.bn_aggr(z_mv[:, t], z_bst[:, t])
                last.then_inc(z_moments, 1)
                dve.wait_ge(z_moments, n)
                nc.vector.tensor_scalar(z_u[:, :], z_mv[:, :, 1], LN_EPS, RMS_EPS ** 2 / C, ALU.add, ALU.mult
                                        ).then_inc(z_u_set, 1)
                nc.vector.tensor_scalar(z_nm[:, :], z_mv[:, :, 0], -1.0, None, ALU.mult)
                dve.wait_ge(z_u_set, n)
                nc.vector.tensor_tensor(z_w[:, :], z_mv[:, :, 1], z_u[:, :], ALU.max).then_inc(z_w_set, 1)

            def zT_rest(b, n):
                dve.wait_ge(zT_hi, n)
                nc.vector.tensor_tensor(zT_all[:, b, LO], zT_ps, zT_all[:, b, HI].bitcast(F32), ALU.subtract
                                        ).then_inc(zT_lo, 1)

            def max_D(b, n):
                dve.wait_ge(LT_mm, n)
                freed(dve, D_exp, b)
                nc.vector.tensor_reduce(nmD[:, :], LT_ps, AX.X, ALU.max, negate=True).then_inc(D_max, 1)

            def max_C(b, n):
                dve.wait_ge(L_mm, n)
                freed(dve, C_exp, b)
                nc.vector.tensor_reduce(nmC[:, :], L_ps, AX.X, ALU.max, negate=True).then_inc(C_max, 1)

            def invert_ZD(b, n):
                dve.wait_ge(D_exp, n)
                freed(dve, Dn_ready, b)
                nc.vector.reciprocal(rZD[:, :], ZD[:, :]).then_inc(ZD_inv, 1)

            def CT_copy(b, n):
                dve.wait_ge(C_turned, n)
                nc.vector.tensor_copy(CT_all[:, b], CT_ps).then_inc(CT_ready, 1)
                nc.vector.reciprocal(rZC_all[:, b], ZC_all[:, b]).then_inc(ZC_inv, 1)

            def slots_rest(b, n):
                dve.wait_ge(slots_hi, n)
                nc.vector.scalar_tensor_tensor(out=slots_all[:, b, LO], in0=slots_ps, scalar=gx_col[:, 0:1],
                                               in1=slots_all[:, b, HI].bitcast(F32), op0=ALU.mult,
                                               op1=ALU.subtract).then_inc(slots_lo, 1)

            def h_rest(g):
                def stage(b, n):
                    dve.wait_ge(h_hi_ready, NG * b + g + 1)
                    freed(dve, PT_mm, NG * b + g - 1)
                    nc.vector.tensor_tensor(h_lo[:, g], h_f[:, g], h_hi[:, g].bitcast(F32), ALU.subtract
                                            ).then_inc(h_lo_ready, 1)
                return stage

            def PT_copy(b, n):
                dve.wait_ge(PT_mm, NG * b + NG)
                freed(dve, P_turned, b)
                nc.vector.tensor_copy(PT_sb[:, :], PT_ps).then_inc(PT_ready, 1)

            def finish(b, n):
                dve.wait_ge(out_mm, n)
                dve.wait_ge(ZC_inv, n)
                dve.wait_ge(x1_saved, 16 * n)
                freed(dve, out_stored, 16 * b)
                for t in range(NT):
                    last = nc.vector.scalar_tensor_tensor(out=out_sb[:, t], in0=out_ps[:, t],
                                                          scalar=rZC_all[:, b, t:t + 1], in1=x1_all[:, b, t],
                                                          op0=ALU.mult, op1=ALU.add)
                last.then_inc(out_ready, 1)

            def before_start():
                x_moments_of(0)
                x_bias(0)

            def before_0():
                split_W1()
                x_moments_of(1)
                x_bias(1)
                dve.wait_ge(ld_rows, 48)

            def before_1():
                x_moments_of(2)
                slot_mean_square()
                x_bias(2)
                slot_normalise()
                dve.wait_ge(mask_set, 3)

            run(dve, [[(-1, mask_scores), (-2, z_sums), (-2, z_variance), (-1, a_sums), (1, xT_rest),
                       (-1, a_centre), (0, v_bias), (-1, residual), (-2, zT_rest)],
                      [(1, max_D), (1, max_C), (1, invert_ZD), (0, CT_copy), (0, slots_rest)],
                      [(1, h_rest(0)), (0, PT_copy), (1, h_rest(1)), (-1, finish)]],
                {(ATTN, -1): before_start, (ATTN, 0): before_0, (ATTN, 1): before_1, (ATTN, 2): slot_rest})

        @block.tensor
        def _(pe):
            def three_pass(dst, stationary, moving, start, stop):
                nc.tensor.matmul(dst, stationary(HI), moving(HI), start=start, stop=False)
                nc.tensor.matmul(dst, stationary(HI), moving(LO), start=False, stop=False)
                return nc.tensor.matmul(dst, stationary(LO), moving(HI), start=False, stop=stop)

            def turn_x(b, n):
                pe.wait_ge(xn_ready, n)
                freed(pe, xT_hi, b)
                freed(pe, xT_lo, b)
                for t in range(NT):
                    last = nc.tensor.transpose(xT_ps[:, t * P:(t + 1) * P], xn[:, t], ident[:, :])
                last.then_inc(x_turned, 1)

            def hidden(b, n):
                pe.wait_ge(xT_hi, n)
                pe.wait_ge(xT_lo, n)
                freed(pe, hid_ready, 3 * b)
                for m in range(3):
                    dst = hqk_ps[:, m] if m < 2 else hv_ps
                    last = three_pass(dst, lambda s: W1_s[:, m, s], lambda s: xT_s[:, s], True, True)
                    if m:
                        last.then_inc(hid_mm, 1)

            def project(b, n):
                freed(pe, qk_ready, 2 * b)
                for m in range(2):
                    pe.wait_ge(hid_ready, 3 * b + m + 1)
                    last = nc.tensor.matmul(qk_ps[:, m], W2_sb[:, m], hidT[:, m], start=True, stop=True)
                last.then_inc(qk_mm, 1)
                pe.wait_ge(hid_ready, 3 * b + 3)
                freed(pe, v_ready, b)
                for t in range(NT):
                    last = nc.tensor.matmul(v_ps[:, t], hidT[:, 2, t * P:(t + 1) * P], W2_sb[:, 2],
                                            start=True, stop=True)
                last.then_inc(v_mm, 1)

            def scores(b, n):
                pe.wait_ge(qk_ready, 2 * b + 2)
                freed(pe, s_ready, b)
                nc.tensor.matmul(s_ps[:, 0:T], qkT[:, 1, 0:P], qkT[:, 0], start=True, stop=True)
                nc.tensor.matmul(s_ps[:, T:SW], qkT[:, 1, P:T], qkT[:, 0, P:T], start=True, stop=True
                                 ).then_inc(s_mm, 1)

            def attend(b, n):
                pe.wait_ge(s_ready, n)
                pe.wait_ge(v_ready, n)
                freed(pe, ac_ready, b)
                nc.tensor.matmul(a_ps[:, 0], sT[:, 0:P], v_sb[:, 0], start=True, stop=True)
                nc.tensor.matmul(a_ps[:, 1], sT[:, P:T], v_sb[:, 0], start=True, stop=False)
                nc.tensor.matmul(a_ps[:, 1], sT[:, T:SW], v_sb[:, 1], start=False, stop=True).then_inc(a_mm, 1)

            def turn_z(b, n):
                pe.wait_ge(z_ready, n)
                freed(pe, zT_hi, b)
                freed(pe, zT_lo, b)
                for t in range(NT):
                    last = nc.tensor.transpose(zT_ps[:, t * P:(t + 1) * P], z_cur[:, t], ident[:, :])
                last.then_inc(z_turned, 1)

            def turn_slots():
                pe.wait_ge(slot_n_set, 1)
                for e in range(NE):
                    last = nc.tensor.transpose(slotT_ps[:, e * P:(e + 1) * P], slot_n[:, e], ident[:, :])
                last.then_inc(slot_turned, 1)

            def logits_T(b, n):
                pe.wait_ge(zT_hi, n)
                pe.wait_ge(zT_lo, n)
                freed(pe, D_exp, b)
                for e in range(NE):
                    last = three_pass(LT_ps[:, e], lambda s: slotT_s[:, s, e * P:(e + 1) * P],
                                      lambda s: zT_all[:, b, s], True, True)
                last.then_inc(LT_mm, 1)

            def logits(b, n):
                pe.wait_ge(zT_staged, 16 * n)
                freed(pe, C_exp, b)
                for t in range(NT):
                    last = three_pass(L_ps[:, t], lambda s: zT_st[:, s, t * P:(t + 1) * P],
                                      lambda s: slotT_s[:, s], True, True)
                last.then_inc(L_mm, 1)

            def turn_D(b, n):
                pe.wait_ge(Dn_ready, n)
                freed(pe, CT_ready, b)
                for t in range(NT):
                    for e in range(NE):
                        last = nc.tensor.transpose(D_ps[:, t, e * P:(e + 1) * P], Dn[:, e, t * P:(t + 1) * P],
                                                   ident[:, :])
                last.then_inc(D_turned, 1)

            def turn_C(b, n):
                pe.wait_ge(C_exp, n)
                pe.wait_ge(D_ready, n)
                for e in range(NE):
                    for t in range(NT):
                        last = nc.tensor.transpose(CT_ps[:, e, t * P:(t + 1) * P], Cx[:, t, e * P:(e + 1) * P],
                                                   ident[:, :])
                last.then_inc(C_turned, 1)

            def slots(b, n):
                pe.wait_ge(D_ready, n)
                pe.wait_ge(z_staged, 16 * n)
                freed(pe, slots_lo, b)
                for t in range(NT):
                    last = nc.tensor.matmul(slots_ps, z_st[:, t], D_sb[:, t], start=(t == 0), stop=(t == NT - 1))
                last.then_inc(slots_mm, 1)

            def expert_hidden(g):
                def stage(b, n):
                    pe.wait_ge(slots_hi, n)
                    pe.wait_ge(slots_lo, n)
                    freed(pe, h_ready, NG * b + g - 1)
                    for j in range(GH):
                        m = g * GH + j
                        last = three_pass(h_ps[g][:, j], lambda s: w1_s[:, s, m * P:(m + 1) * P],
                                          lambda s: slots_all[:, b, s], True, True)
                    last.then_inc(h_mm, 1)
                return stage

            def expert_out(g):
                def stage(b, n):
                    pe.wait_ge(h_hi_ready, NG * b + g + 1)
                    pe.wait_ge(h_lo_ready, NG * b + g + 1)
                    if g == 0:
                        freed(pe, PT_ready, b)
                    for j in range(GH):
                        m = g * GH + j
                        last = three_pass(PT_ps, lambda s: w2_s[:, s, m],
                                          lambda s: (h_hi, h_lo)[s][:, g, j], m == 0, m == NH - 1)
                    last.then_inc(PT_mm, 1)
                return stage

            def turn_P(b, n):
                pe.wait_ge(PT_ready, n)
                freed(pe, P_ready, b)
                for e in range(NE):
                    last = nc.tensor.transpose(P_ps[:, e], PT_sb[:, e * P:(e + 1) * P], ident[:, :])
                last.then_inc(P_turned, 1)

            def combine(b, n):
                pe.wait_ge(P_ready, n)
                pe.wait_ge(CT_staged, 16 * n)
                freed(pe, out_ready, b)
                for t in range(NT):
                    for e in range(NE):
                        last = nc.tensor.matmul(out_ps[:, t], CT_st[:, e, t * P:(t + 1) * P], P_sb[:, e],
                                                start=(e == 0), stop=(e == NE - 1))
                last.then_inc(out_mm, 1)

            def weights_in():
                pe.wait_ge(W1_split, 2)
                pe.wait_ge(ld_W2, 48)

            def attention_left_1_to_4():
                pe.wait_ge(hid_ready, 3 * B)
                pe.wait_ge(qk_ready, 2 * B)
                pe.wait_ge(v_ready, B)

            def attention_left_the_rest():
                pe.wait_ge(xT_lo, B)
                pe.wait_ge(s_ready, B)
                pe.wait_ge(ac_ready, B)

            def routing_left_1_to_4():
                pe.wait_ge(C_exp, B)
                pe.wait_ge(D_exp, B)
                pe.wait_ge(w_split, 4)

            def routing_left_the_rest():
                pe.wait_ge(CT_ready, B)
                pe.wait_ge(zT_lo, B)

            run(pe, [[(0, hidden), (-1, attend), (1, turn_x), (0, project), (-2, turn_z), (0, scores)],
                     [(1, logits_T), (0, turn_D), (1, logits), (0, slots), (0, turn_C)],
                     [(1, expert_hidden(0)), (0, expert_out(0)), (1, expert_hidden(1)), (0, expert_out(1)),
                      (-1, combine), (0, turn_P)]],
                {(ATTN, -1): lambda: pe.wait_ge(ident_set, 2), (ATTN, 0): weights_in, (ATTN, 1): turn_slots,
                 (ATTN, 2): lambda: pe.wait_ge(slotT_lo, 1), (ROUTE, -1): attention_left_1_to_4,
                 (ROUTE, 0): attention_left_the_rest, (EXPERT, -1): routing_left_1_to_4,
                 (EXPERT, 0): routing_left_the_rest})


_INS = ['L0_attn_x', 'L0_attn_W1q', 'L0_attn_b1q', 'L0_attn_W2q', 'L0_attn_b2q', 'L0_attn_W1k', 'L0_attn_b1k',
        'L0_attn_W2k', 'L0_attn_b2k', 'L0_attn_W1v', 'L0_attn_b1v', 'L0_attn_W2v', 'L0_attn_b2v', 'L0_attn_ln_w',
        'L0_attn_ln_b', 'L0_ffn_gamma_x', 'L0_ffn_gamma_slot', 'L0_ffn_slot_embeds', 'L0_ffn_w1', 'L0_ffn_w2']
_OUTS = [((8, 256, 128), 'float32')]


def kernel(**inputs):
    import numpy as _np
    import concourse.bacc as _bacc
    from concourse import mybir as _mybir
    from concourse.bass_utils import run_bass_kernel_spmd as _run

    nc = _bacc.Bacc("TRN2", target_bir_lowering=False, num_devices=1)
    arrays, args = {}, []
    for name in _INS:
        a = _np.ascontiguousarray(inputs[name])
        arrays[f"in_{name}_dram"] = a
        args.append(nc.dram_tensor(f"in_{name}_dram", a.shape, _mybir.dt.from_np(a.dtype), kind="ExternalInput").ap())
    for i, (shape, dtype) in enumerate(_OUTS):
        dt = _mybir.dt.from_np(_np.dtype(dtype))
        args.append(nc.dram_tensor(f"out_{i}_dram", shape, dt, kind="ExternalOutput").ap())
    build(nc, *args)
    r = _run(nc, [arrays], core_ids=[0])
    got = tuple(r.results[0][f"out_{i}_dram"] for i in range(len(_OUTS)))
    return got[0]
```

```python
from contextlib import ExitStack

import concourse.bass as bass
from concourse import mybir

F32 = mybir.dt.float32
F32R = mybir.dt.float32r
ALU = mybir.AluOpType
ACT = mybir.ActivationFunctionType
AX = mybir.AxisListType

LN_EPS = 1e-5
RMS_EPS = 1e-12
HI, LO = 0, 1
ATTN, INTO_ROUTE, ROUTE, INTO_EXPERT, EXPERT = range(5)


def build(nc, x, W1q, b1q, W2q, b2q, W1k, b1k, W2k, b2k, W1v, b1v, W2v, b2v, ln_w, ln_b,
          gamma_x, gamma_slot, slot_embeds, w1, w2, out):
    B, T, C = x.shape
    P = 128
    NT = T // P
    E = slot_embeds.shape[0] * slot_embeds.shape[1]
    NE = E // P
    HID = w1.shape[1]
    NH = HID // P
    NG = 2
    GH = NH // NG
    assert C == P and NT == 2 and NE == 4 and NH == 4
    inv_scale = 1.0 / float((C * T) ** 0.5)
    SW = T + P
    X_GROUPS = [(0, 1), (1, 3), (3, 5), (5, B)]

    x_v = x.rearrange("b (t p) c -> p b t c", p=P)
    out_v = out.rearrange("b (t p) c -> p b t c", p=P)

    ctx = ExitStack()
    with ctx:
        def sb(name, shape, dt=F32):
            return ctx.enter_context(nc.sbuf_tensor(name, [P] + list(shape), dt))

        def sem(name):
            return ctx.enter_context(nc.semaphore(name))

        x_sb = sb("x_sb", [B, NT, C])
        W1_raw = sb("W1_raw", [3, C])
        W1_s = sb("W1_s", [3, 2, C], F32R)
        W2_sb = sb("W2_sb", [3, C])
        b1_col = sb("b1_col", [3])
        b2_col = sb("b2_col", [2])
        b2v_row = sb("b2v_row", [C])
        lnw_row = sb("lnw_row", [C])
        lnb_row = sb("lnb_row", [C])
        gx_col = sb("gx_col", [1])
        gs_col = sb("gs_col", [1])
        gg_col = sb("gg_col", [1])
        slot_raw = sb("slot_raw", [NE, C])
        slot_sq = sb("slot_sq", [NE, C])
        slot_n = sb("slot_n", [NE, C])
        slot_ss = sb("slot_ss", [NE])
        slot_ms = sb("slot_ms", [NE])
        slot_r = sb("slot_r", [NE])
        slotT_s = sb("slotT_s", [2, E], F32R)
        w1_raw = sb("w1_raw", [HID])
        w1_s = sb("w1_s", [2, HID], F32R)
        w2_raw = sb("w2_raw", [NH, C])
        w2_s = sb("w2_s", [2, NH, C], F32R)
        ident = sb("ident", [P])
        mask = sb("mask", [SW])
        minus_half = sb("minus_half", [B * NT])
        gelu_warm = sb("gelu_warm", [1])

        x_bst = sb("x_bst", [B, NT, 6])
        x_mv = sb("x_mv", [B, NT, 2])
        x_ve = sb("x_ve", [B * NT])
        x_rs = sb("x_rs", [B * NT])
        x_nb = sb("x_nb", [B * NT])
        xn = sb("xn", [NT, C])
        xT_s = sb("xT_s", [2, T], F32R)
        hidT = sb("hidT", [3, T])
        qkT = sb("qkT", [2, T])
        v_sb = sb("v_sb", [NT, C])
        sT = sb("sT", [SW])
        a_bst = sb("a_bst", [NT, 6])
        a_mv = sb("a_mv", [NT, 2])
        a_ve = sb("a_ve", [NT])
        a_rs = sb("a_rs", [NT])
        ac = sb("ac", [NT, C])
        xb = sb("xb", [NT, C])
        x1_cur = sb("x1_cur", [NT, C])
        z_bst = sb("z_bst", [NT, 6])
        z_mv = sb("z_mv", [NT, 2])
        z_nm = sb("z_nm", [NT])
        z_u = sb("z_u", [NT])
        z_w = sb("z_w", [NT])
        z_rs = sb("z_rs", [NT])
        z_cur = sb("z_cur", [NT, C])

        x1_all = sb("x1_all", [B, NT, C])
        z_all = sb("z_all", [B, NT, C])
        zT_all = sb("zT_all", [B, 2, T], F32R)
        slots_all = sb("slots_all", [B, 2, E], F32R)
        CT_all = sb("CT_all", [B, NE, T])
        ZC_all = sb("ZC_all", [B, NT])
        rZC_all = sb("rZC_all", [B, NT])

        z_st = sb("z_st", [NT, C])
        zT_st = sb("zT_st", [2, T], F32R)
        nmC = sb("nmC", [NT])
        nmD = sb("nmD", [NE])
        ZD = sb("ZD", [NE])
        rZD = sb("rZD", [NE])
        Cx = sb("Cx", [NT, E])
        Dx = sb("Dx", [NE, T])
        Dn = sb("Dn", [NE, T])
        D_sb = sb("D_sb", [NT, E])

        CT_st = sb("CT_st", [NE, T])
        h_f = sb("h_f", [NG, GH, E])
        h_hi = sb("h_hi", [NG, GH, E], F32R)
        h_lo = sb("h_lo", [NG, GH, E], F32R)
        PT_sb = sb("PT_sb", [E])
        P_sb = sb("P_sb", [NE, C])
        out_sb = sb("out_sb", [NT, C])

        ps = ctx.enter_context(nc.psum_tensor("ps", [P, 8, 512], F32))
        xT_ps = ps[:, 0, 0:T]
        hqk_ps = ps[:, 1, :].rearrange("p (m t) -> p m t", m=2)
        hv_ps = ps[:, 2, 0:T]
        qk_ps = ps[:, 3, :].rearrange("p (m t) -> p m t", m=2)
        v_ps = ps[:, 4, 0:NT * C].rearrange("p (t c) -> p t c", t=NT)
        s_ps = ps[:, 5, 0:SW]
        a_ps = ps[:, 6, 0:NT * C].rearrange("p (t c) -> p t c", t=NT)
        zT_ps = ps[:, 7, 0:T]
        slotT_ps = ps[:, 0, :]
        L_ps = ps[:, 1:3, :]
        LT_ps = ps[:, 3:5, :].rearrange("p k (e t) -> p (k e) t", e=2)
        D_ps = ps[:, 5:7, :]
        CT_ps = ps[:, 5:7, :].rearrange("p k (e t) -> p (k e) t", e=2)
        slots_ps = ps[:, 0, :]
        h_ps = [ps[:, 3:5, :], ps[:, 1:3, :]]
        PT_ps = ps[:, 7, :]
        P_ps = ps[:, 5, :].rearrange("p (e c) -> p e c", e=NE)
        out_ps = ps[:, 6, 0:NT * C].rearrange("p (t c) -> p t c", t=NT)

        ld_x = [sem(f"ld_x{g}") for g in range(len(X_GROUPS))]
        ld_W1, ld_W2, ld_b1, ld_b2, ld_rows, ld_slot, ld_w = (
            sem("ld_W1"), sem("ld_W2"), sem("ld_b1"), sem("ld_b2"), sem("ld_rows"), sem("ld_slot"),
            sem("ld_w"))
        ident_set, mask_set, half_set, gelu_warmed = (
            sem("ident_set"), sem("mask_set"), sem("half_set"), sem("gelu_warmed"))
        W1_split, w_hi, w_lo, gg_set = sem("W1_split"), sem("w_hi"), sem("w_lo"), sem("gg_set")
        slot_sq_done, slot_ms_set, slot_r_set, slot_n_set = (
            sem("slot_sq_done"), sem("slot_ms_set"), sem("slot_r_set"), sem("slot_n_set"))
        slot_turned, slotT_hi, slotT_lo = sem("slot_turned"), sem("slotT_hi"), sem("slotT_lo")

        x_stats, x_moments, x_eps, x_rstd, x_nb_set = (
            sem("x_stats"), sem("x_moments"), sem("x_eps"), sem("x_rstd"), sem("x_nb_set"))
        xn_ready, x_turned, xT_hi, xT_lo = sem("xn_ready"), sem("x_turned"), sem("xT_hi"), sem("xT_lo")
        hid_mm, hid_ready = sem("hid_mm"), sem("hid_ready")
        qk_mm, qk_ready, v_mm, v_ready = sem("qk_mm"), sem("qk_ready"), sem("v_mm"), sem("v_ready")
        s_mm, s_ready, a_mm = sem("s_mm"), sem("s_ready"), sem("a_mm")
        a_stats, a_moments, a_eps, a_rstd, ac_ready = (
            sem("a_stats"), sem("a_moments"), sem("a_eps"), sem("a_rstd"), sem("ac_ready"))
        xb_ready, x1_ready = sem("xb_ready"), sem("x1_ready")
        z_stats, z_moments, z_u_set, z_w_set, z_rstd, z_ready = (
            sem("z_stats"), sem("z_moments"), sem("z_u_set"), sem("z_w_set"), sem("z_rstd"), sem("z_ready"))
        x1_saved, z_saved = sem("x1_saved"), sem("z_saved")
        z_turned, zT_hi, zT_lo = sem("z_turned"), sem("zT_hi"), sem("zT_lo")

        z_staged, zT_staged = sem("z_staged"), sem("zT_staged")
        LT_mm, L_mm, D_max, C_max = sem("LT_mm"), sem("L_mm"), sem("D_max"), sem("C_max")
        D_exp, C_exp, ZD_inv, ZC_inv, Dn_ready = (
            sem("D_exp"), sem("C_exp"), sem("ZD_inv"), sem("ZC_inv"), sem("Dn_ready"))
        D_turned, D_ready, C_turned, CT_ready = sem("D_turned"), sem("D_ready"), sem("C_turned"), sem("CT_ready")
        slots_mm, slots_hi, slots_lo = sem("slots_mm"), sem("slots_hi"), sem("slots_lo")

        CT_staged = sem("CT_staged")
        h_mm, h_ready, h_hi_ready, h_lo_ready, PT_mm = (
            sem("h_mm"), sem("h_ready"), sem("h_hi_ready"), sem("h_lo_ready"), sem("PT_mm"))
        PT_ready, P_turned, P_ready, out_mm, out_ready = (
            sem("PT_ready"), sem("P_turned"), sem("P_ready"), sem("out_mm"), sem("out_ready"))
        out_stored = sem("out_stored")

        block = ctx.enter_context(nc.Block())

        SCHEDULE = [(ATTN, -1, 4), (ATTN, 4, B - 1), (ATTN, B - 1, B), (INTO_ROUTE, -1, 2), (ROUTE, 2, B - 2),
                    (ROUTE, B - 2, B - 1), (INTO_EXPERT, B - 1, B), (EXPERT, 0, 2), (EXPERT, 2, B - 1),
                    (EXPERT, B - 1, B + 1)]
        LOOPS = [(ATTN, 4, B - 1), (ROUTE, 2, B - 2), (EXPERT, 2, B - 1)]
        LATE = B + 1
        FIRST = 1 - B

        def run(eng, phases, before):
            for part in SCHEDULE:
                phase, k0, k1 = part
                stages = phases[phase]
                if part in LOOPS:
                    before.get((phase, k0), lambda: None)()
                    if not stages:
                        continue
                    offsets = [o for o, _ in stages]
                    with eng.Fori(k0, k1) as k:
                        at = {o: in_register(eng, k + o, k0 + o, k1 - 1 + o) for o in range(min(offsets), max(offsets) + 2)}
                        for o, stage in stages:
                            stage(at[o], at[o + 1])
                else:
                    for k in range(k0, k1):
                        before.get((phase, k), lambda: None)()
                        for o, stage in stages:
                            if 0 <= k + o < B:
                                stage(k + o, k + o + 1)

        def in_register(eng, value, least, most):
            return eng.snap(eng.to_reg(value), min_val=least, max_val=most)

        def first_batch(b):
            return isinstance(b, int) and b == 0

        def last_batch(b):
            return isinstance(b, int) and b == B - 1

        def freed(eng, semaphore, count):
            if not (isinstance(count, int) and count <= 0):
                eng.wait_ge(semaphore, count)

        def own_instruction(eng):
            eng.wait_ge(half_set, 1)

        @block.sync
        def _(sp):
            sp.dma_start(x_sb[:, 0], x_v[:, 0]).then_inc(ld_x[0], 16)
            for m, W in enumerate((W1q, W1k, W1v)):
                sp.dma_start(W1_raw[:, m], W).then_inc(ld_W1, 16)
            sp.dma_start(x_sb[:, 1:3], x_v[:, 1:3]).then_inc(ld_x[1], 16)
            for m, b in enumerate((b1q, b1k, b1v)):
                sp.dma_start(b1_col[:, m:m + 1], b[:, None]).then_inc(ld_b1, 16)
            sp.dma_start(x_sb[:, 3:5], x_v[:, 3:5]).then_inc(ld_x[2], 16)
            for m, W in enumerate((W2q, W2k, W2v)):
                sp.dma_start(W2_sb[:, m], W).then_inc(ld_W2, 16)
            for m, b in enumerate((b2q, b2k)):
                sp.dma_start(b2_col[:, m:m + 1], b[:, None]).then_inc(ld_b2, 16)
            sp.dma_start(x_sb[:, 5:B], x_v[:, 5:B]).then_inc(ld_x[3], 16)
            sp.dma_start(w1_raw[:, :], w1).then_inc(ld_w, 16)
            sp.dma_start(w2_raw[:, :, :], w2.rearrange("(k p) c -> p k c", p=P)).then_inc(ld_w, 16)

            def save_x1(b, n):
                own_instruction(sp)
                sp.wait_ge(x1_ready, n)
                sp.dma_start(x1_all[:, b], x1_cur[:, :, :]).then_inc(x1_saved, 16)

            def save_z(b, n):
                own_instruction(sp)
                sp.wait_ge(z_ready, n)
                sp.dma_start(z_all[:, b], z_cur[:, :, :]).then_inc(z_saved, 16)

            def stage_zT(b, n):
                own_instruction(sp)
                sp.wait_ge(zT_hi, n)
                sp.wait_ge(zT_lo, n)
                freed(sp, L_mm, b)
                sp.dma_start(zT_st[:, :, :].bitcast(F32), zT_all[:, b].bitcast(F32)).then_inc(zT_staged, 16)

            def stage_z(b, n):
                landed = 16 * n if isinstance(n, int) else in_register(sp, 16 * n, 16, 16 * B)
                own_instruction(sp)
                sp.wait_ge(z_saved, landed)
                freed(sp, slots_mm, b)
                sp.dma_start(z_st[:, :, :], z_all[:, b]).then_inc(z_staged, 16)

            def stage_CT(b, n):
                if last_batch(b):
                    return
                own_instruction(sp)
                sp.wait_ge(CT_ready, n)
                freed(sp, out_mm, b)
                sp.dma_start(CT_st[:, :, :], CT_all[:, b]).then_inc(CT_staged, 16)

            def store(b, n):
                own_instruction(sp)
                sp.wait_ge(out_ready, n)
                sp.dma_start(out_v[:, b], out_sb[:, :, :]).then_inc(out_stored, 16)

            run(sp, [[(-2, save_x1), (-2, save_z)],
                     [(LATE - 2, save_x1), (2, stage_zT), (1, stage_z), (LATE - 2, save_z)],
                     [(2, stage_zT), (1, stage_z)],
                     [],
                     [(0, stage_CT), (-1, store)]],
                {(ATTN, B - 1): lambda: stage_zT(0, 1)})
            sp.wait_ge(out_stored, 16 * B)

        @block.gpsimd
        def _(pool):
            nc.gpsimd.memset(minus_half[:, :], -0.5).then_inc(half_set, 1)
            nc.gpsimd.memset(ident[:, :], 0.0).then_inc(ident_set, 1)
            nc.gpsimd.memset(mask[:, :], inv_scale).then_inc(mask_set, 1)
            pool.wait_ge(ident_set, 1)
            nc.gpsimd.affine_select(out=ident[:, :], in_=ident[:, :], compare_op=ALU.not_equal, fill=1.0,
                                    base=0, pattern=[[-1, P]], channel_multiplier=1).then_inc(ident_set, 1)
            for row, b in ((b2v_row, b2v), (lnw_row, ln_w)):
                pool.dma_start(row[:, :], b.partition_broadcast(P)).then_inc(ld_rows, 16)

            def load_slots():
                pool.dma_start(slot_raw[:, :, :],
                               slot_embeds.rearrange("e t c -> (e t) c").rearrange("(k p) c -> p k c", p=P)
                               ).then_inc(ld_slot, 16)
                pool.dma_start(gx_col[:, :], gamma_x[:, None]).then_inc(ld_slot, 16)
                pool.dma_start(gs_col[:, :], gamma_slot[:, None]).then_inc(ld_slot, 16)

            def mask_triangles():
                pool.wait_ge(mask_set, 1)
                for c0 in (0, T):
                    tri = mask[:, c0:c0 + P]
                    nc.gpsimd.affine_select(out=tri, in_=tri, compare_op=ALU.is_ge, fill=0.0, base=0,
                                            pattern=[[1, P]], channel_multiplier=-1).then_inc(mask_set, 1)

            def x_rsqrt(g):
                b0, b1 = X_GROUPS[g]
                cols = slice(b0 * NT, b1 * NT)
                pool.wait_ge(half_set, 1)
                pool.wait_ge(x_moments, g + 1)
                nc.gpsimd.tensor_scalar(x_ve[:, cols], x_mv[:, b0:b1, :, 1].rearrange("p b t -> p (b t)"),
                                        LN_EPS, 1.0, ALU.add, ALU.mult).then_inc(x_eps, 1)
                pool.wait_ge(x_eps, g + 1)
                nc.gpsimd.tensor_tensor(x_rs[:, cols], x_ve[:, cols], minus_half[:, 0:(b1 - b0) * NT], ALU.pow
                                        ).then_inc(x_rstd, 1)

            def slot_rsqrt():
                pool.wait_ge(slot_ms_set, 1)
                nc.gpsimd.tensor_tensor(slot_r[:, :], slot_ms[:, :], minus_half[:, 0:NE], ALU.pow
                                        ).then_inc(slot_r_set, 1)

            def experts_rest(i, w_s, w_raw):
                pool.wait_ge(w_hi, i + 1)
                nc.gpsimd.tensor_tensor(w_s[:, LO], w_raw, w_s[:, HI].bitcast(F32), ALU.subtract).then_inc(w_lo, 1)

            def x_plus_bias(b, n):
                freed(pool, x1_ready, b)
                nc.gpsimd.tensor_tensor(xb[:, :, :], x_sb[:, b],
                                        lnb_row[:, :].unsqueeze(1).to_broadcast([P, NT, C]), ALU.add
                                        ).then_inc(xb_ready, 1)

            def a_rsqrt(b, n):
                own_instruction(pool)
                pool.wait_ge(a_moments, n)
                nc.gpsimd.tensor_scalar(a_ve[:, :], a_mv[:, :, 1], LN_EPS, 1.0, ALU.add, ALU.mult
                                        ).then_inc(a_eps, 1)
                pool.wait_ge(a_eps, n)
                freed(pool, x1_ready, b)
                nc.gpsimd.tensor_tensor(a_rs[:, :], a_ve[:, :], minus_half[:, 0:NT], ALU.pow).then_inc(a_rstd, 1)

            def z_rsqrt(b, n):
                pool.wait_ge(z_w_set, n)
                nc.gpsimd.tensor_tensor(z_rs[:, :], z_w[:, :], minus_half[:, 0:NT], ALU.pow).then_inc(z_rstd, 1)

            def z_normalise(b, n):
                landed = 16 * b if isinstance(b, int) else in_register(pool, 16 * b, 16, 16 * B)
                own_instruction(pool)
                pool.wait_ge(z_rstd, n)
                freed(pool, z_turned, b)
                freed(pool, z_saved, landed)
                for t in range(NT):
                    last = nc.gpsimd.tensor_scalar(z_cur[:, t], x1_cur[:, t], z_nm[:, t:t + 1], z_rs[:, t:t + 1],
                                                   ALU.add, ALU.mult)
                last.then_inc(z_ready, 1)

            def D_normalise(b, n):
                own_instruction(pool)
                pool.wait_ge(ZD_inv, n)
                freed(pool, D_turned, b)
                for e in range(NE):
                    last = nc.gpsimd.tensor_scalar(Dn[:, e], Dx[:, e], rZD[:, e:e + 1], 1.0, ALU.mult, ALU.mult)
                last.then_inc(Dn_ready, 1)

            def before_start():
                x_rsqrt(0)
                pool.dma_start(lnb_row[:, :], ln_b.partition_broadcast(P)).then_inc(ld_rows, 16)

            def before_0():
                x_rsqrt(1)
                mask_triangles()

            def before_1():
                pool.wait_ge(ld_rows, 48)
                load_slots()
                x_rsqrt(2)

            def before_2():
                experts_rest(0, w1_s, w1_raw[:, :])
                x_rsqrt(3)

            run(pool, [[(-1, x_plus_bias), (-2, z_rsqrt), (-2, z_normalise), (-1, a_rsqrt)],
                       [(LATE - 1, x_plus_bias), (LATE - 2, z_rsqrt), (LATE - 2, z_normalise), (LATE - 1, a_rsqrt),
                        (1, D_normalise)],
                       [(1, D_normalise)], [], []],
                {(ATTN, -1): before_start, (ATTN, 0): before_0, (ATTN, 1): before_1, (ATTN, 2): before_2,
                 (ATTN, 3): slot_rsqrt, (ATTN, B - 1): lambda: experts_rest(1, w2_s, w2_raw[:, :, :])})

        @block.scalar
        def _(act):
            act.wait_ge(half_set, 1)
            nc.scalar.activation(gelu_warm[:, :], minus_half[:, 0:1], ACT.Gelu).then_inc(gelu_warmed, 1)

            def x_group(g):
                act.wait_ge(ld_x[g], 16)
                act.wait_ge(x_rstd, g + 1)
                act.wait_ge(x_nb_set, g + 1)

            def x_normalise(b, n):
                freed(act, x_turned, b)
                for t in range(NT):
                    last = nc.scalar.activation(xn[:, t], x_sb[:, b, t], ACT.Identity,
                                                bias=x_nb[:, bass.ds(b * NT + t, 1)],
                                                scale=x_rs[:, bass.ds(b * NT + t, 1)])
                last.then_inc(xn_ready, 1)

            def hidden_qk(b, n):
                freed(act, v_mm, b)
                act.wait_ge(hid_mm, 2 * b + 1)
                for m in range(2):
                    nc.scalar.activation(hidT[:, m], hqk_ps[:, m], ACT.Gelu, bias=b1_col[:, m:m + 1]
                                         ).then_inc(hid_ready, 1)

            def hidden_v(b, n):
                act.wait_ge(hid_mm, 2 * b + 2)
                nc.scalar.activation(hidT[:, 2], hv_ps, ACT.Gelu, bias=b1_col[:, 2:3]).then_inc(hid_ready, 1)

            def xT_round(b, n):
                act.wait_ge(x_turned, n)
                freed(act, hid_mm, 2 * b)
                nc.scalar.copy(xT_s[:, HI], xT_ps).then_inc(xT_hi, 1)

            def qk(b, n):
                act.wait_ge(qk_mm, n)
                freed(act, s_mm, b)
                for m in range(2):
                    nc.scalar.activation(qkT[:, m], qk_ps[:, m], ACT.Identity, bias=b2_col[:, m:m + 1]
                                         ).then_inc(qk_ready, 1)

            def zT_round(b, n):
                act.wait_ge(z_turned, n)
                nc.scalar.copy(zT_all[:, b, HI], zT_ps).then_inc(zT_hi, 1)

            def round_experts():
                act.wait_ge(ld_w, 32)
                nc.scalar.copy(w1_s[:, HI], w1_raw[:, :]).then_inc(w_hi, 1)
                nc.scalar.copy(w2_s[:, HI], w2_raw[:, :, :]).then_inc(w_hi, 1)

            def slot_squares():
                act.wait_ge(ld_slot, 48)
                for e in range(NE):
                    nc.scalar.activation(slot_sq[:, e], slot_raw[:, e], ACT.Square,
                                         accum_out=slot_ss[:, e:e + 1]).then_inc(slot_sq_done, 1)

            def slot_round():
                act.wait_ge(slot_turned, 1)
                act.wait_ge(gg_set, 1)
                nc.scalar.activation(slotT_s[:, HI], slotT_ps, ACT.Identity, scale=gg_col[:, 0:1]
                                     ).then_inc(slotT_hi, 1)

            def D_back(b, n):
                act.wait_ge(D_turned, n)
                freed(act, slots_mm, b)
                nc.scalar.copy(D_sb[:, :, :], D_ps).then_inc(D_ready, 1)

            def exp_D(b, n):
                act.wait_ge(D_max, n)
                freed(act, Dn_ready, b)
                freed(act, ZD_inv, b)
                for e in range(NE):
                    last = nc.scalar.activation(Dx[:, e], LT_ps[:, e], ACT.Exp, bias=nmD[:, e:e + 1],
                                                accum_out=ZD[:, e:e + 1])
                last.then_inc(D_exp, 1)

            def slots_round(b, n):
                act.wait_ge(slots_mm, n)
                nc.scalar.activation(slots_all[:, b, HI], slots_ps, ACT.Identity, scale=gx_col[:, 0:1]
                                     ).then_inc(slots_hi, 1)

            def exp_C(b, n):
                act.wait_ge(C_max, n)
                freed(act, C_turned, b)
                for t in range(NT):
                    last = nc.scalar.activation(Cx[:, t], L_ps[:, t], ACT.Exp, bias=nmC[:, t:t + 1],
                                                accum_out=ZC_all[:, b, t:t + 1])
                last.then_inc(C_exp, 1)

            def gelu_group(g):
                def stage(b, n):
                    act.wait_ge(h_mm, NG * b + g + 1)
                    freed(act, h_lo_ready, NG * b + g - 1)
                    nc.scalar.activation(h_f[:, g], h_ps[g], ACT.Gelu).then_inc(h_ready, 1)
                    act.wait_ge(h_ready, NG * b + g + 1)
                    freed(act, PT_mm, NG * b + g - 1)
                    nc.scalar.copy(h_hi[:, g], h_f[:, g]).then_inc(h_hi_ready, 1)
                return stage

            def P_copy(b, n):
                act.wait_ge(P_turned, n)
                freed(act, out_mm, b)
                nc.scalar.copy(P_sb[:, :, :], P_ps).then_inc(P_ready, 1)

            def before_0():
                x_group(1)
                act.wait_ge(ld_b1, 48)
                act.wait_ge(ld_b2, 32)

            def before_2():
                slot_squares()
                x_group(2)

            def fetch_gelu():
                nc.scalar.activation(gelu_warm[:, :], minus_half[:, 0:1], ACT.Gelu).then_inc(gelu_warmed, 1)

            run(act, [[(1, x_normalise), (0, hidden_qk), (0, hidden_v), (-3, zT_round), (1, xT_round), (0, qk)],
                      [(LATE - 3, zT_round), (0, D_back), (1, exp_D), (0, slots_round), (1, exp_C)],
                      [(0, D_back), (1, exp_D), (0, slots_round), (1, exp_C)],
                      [(0, D_back), (FIRST, gelu_group(0)), (0, slots_round), (FIRST, gelu_group(1))],
                      [(1, gelu_group(0)), (1, gelu_group(1)), (0, P_copy)]],
                {(ATTN, -1): lambda: x_group(0), (ATTN, 0): before_0, (ATTN, 1): round_experts, (ATTN, 2): before_2,
                 (ATTN, 4): lambda: x_group(3), (ATTN, B - 1): slot_round, (INTO_EXPERT, B - 1): fetch_gelu})

        @block.vector
        def _(dve):
            def x_moments_of(g):
                b0, b1 = X_GROUPS[g]
                dve.wait_ge(ld_x[g], 16)
                for b in range(b0, b1):
                    for t in range(NT):
                        last = nc.vector.bn_stats(x_bst[:, b, t], x_sb[:, b, t])
                last.then_inc(x_stats, 1)
                dve.wait_ge(x_stats, g + 1)
                for b in range(b0, b1):
                    for t in range(NT):
                        last = nc.vector.bn_aggr(x_mv[:, b, t], x_bst[:, b, t])
                last.then_inc(x_moments, 1)

            def x_bias(g):
                b0, b1 = X_GROUPS[g]
                cols = slice(b0 * NT, b1 * NT)
                dve.wait_ge(x_moments, g + 1)
                dve.wait_ge(x_rstd, g + 1)
                nc.vector.scalar_tensor_tensor(out=x_nb[:, cols],
                                               in0=x_mv[:, b0:b1, :, 0].rearrange("p b t -> p (b t)"), scalar=-1.0,
                                               in1=x_rs[:, cols], op0=ALU.mult, op1=ALU.mult).then_inc(x_nb_set, 1)

            def split_W1():
                dve.wait_ge(ld_W1, 48)
                nc.vector.tensor_copy(W1_s[:, :, HI], W1_raw[:, :, :]).then_inc(W1_split, 1)
                dve.wait_ge(W1_split, 1)
                nc.vector.tensor_tensor(W1_s[:, :, LO], W1_raw[:, :, :], W1_s[:, :, HI].bitcast(F32),
                                        ALU.subtract).then_inc(W1_split, 1)

            def slot_mean_square():
                dve.wait_ge(slot_sq_done, NE)
                nc.vector.tensor_scalar(slot_ms[:, :], slot_ss[:, :], 1.0 / C, RMS_EPS ** 2 / C,
                                        ALU.mult, ALU.max).then_inc(slot_ms_set, 1)
                dve.wait_ge(ld_slot, 48)
                nc.vector.tensor_tensor(gg_col[:, :], gx_col[:, :], gs_col[:, :], ALU.mult).then_inc(gg_set, 1)

            def slot_normalise():
                dve.wait_ge(slot_r_set, 1)
                for e in range(NE):
                    last = nc.vector.tensor_scalar(slot_n[:, e], slot_raw[:, e], slot_r[:, e:e + 1], None, ALU.mult)
                last.then_inc(slot_n_set, 1)

            def slot_rest():
                dve.wait_ge(slotT_hi, 1)
                nc.vector.scalar_tensor_tensor(out=slotT_s[:, LO], in0=slotT_ps, scalar=gg_col[:, 0:1],
                                               in1=slotT_s[:, HI].bitcast(F32), op0=ALU.mult, op1=ALU.subtract
                                               ).then_inc(slotT_lo, 1)

            def xT_rest(b, n):
                dve.wait_ge(xT_hi, n)
                freed(dve, hid_mm, 2 * b)
                nc.vector.tensor_tensor(xT_s[:, LO], xT_ps, xT_s[:, HI].bitcast(F32), ALU.subtract
                                        ).then_inc(xT_lo, 1)

            def v_bias(b, n):
                dve.wait_ge(v_mm, n)
                freed(dve, a_mm, b)
                nc.vector.tensor_tensor(v_sb[:, :, :], v_ps,
                                        b2v_row[:, :].unsqueeze(1).to_broadcast([P, NT, C]), ALU.add
                                        ).then_inc(v_ready, 1)

            def mask_scores(b, n):
                dve.wait_ge(s_mm, n)
                freed(dve, a_mm, b)
                nc.vector.tensor_tensor(sT[:, :], s_ps, mask[:, :], ALU.mult).then_inc(s_ready, 1)

            def a_sums(b, n):
                dve.wait_ge(a_mm, n)
                for t in range(NT):
                    last = nc.vector.bn_stats(a_bst[:, t], a_ps[:, t])
                last.then_inc(a_stats, 1)

            def a_centre(b, n):
                own_instruction(dve)
                dve.wait_ge(a_stats, n)
                freed(dve, a_rstd, b)
                for t in range(NT):
                    last = nc.vector.bn_aggr(a_mv[:, t], a_bst[:, t])
                last.then_inc(a_moments, 1)
                dve.wait_ge(a_moments, n)
                freed(dve, x1_ready, b)
                for t in range(NT):
                    last = nc.vector.scalar_tensor_tensor(out=ac[:, t], in0=a_ps[:, t], scalar=a_mv[:, t, 0:1],
                                                          in1=lnw_row[:, :], op0=ALU.subtract, op1=ALU.mult)
                last.then_inc(ac_ready, 1)

            def residual(b, n):
                dve.wait_ge(a_rstd, n)
                dve.wait_ge(ac_ready, n)
                dve.wait_ge(xb_ready, n)
                freed(dve, z_ready, b)
                freed(dve, x1_saved, 16 * b)
                for t in range(NT):
                    last = nc.vector.scalar_tensor_tensor(out=x1_cur[:, t], in0=ac[:, t], scalar=a_rs[:, t:t + 1],
                                                          in1=xb[:, t], op0=ALU.mult, op1=ALU.add)
                last.then_inc(x1_ready, 1)

            def z_sums(b, n):
                dve.wait_ge(x1_ready, n)
                for t in range(NT):
                    last = nc.vector.bn_stats(z_bst[:, t], x1_cur[:, t])
                last.then_inc(z_stats, 1)

            def z_variance(b, n):
                own_instruction(dve)
                dve.wait_ge(z_stats, n)
                freed(dve, z_ready, b)
                for t in range(NT):
                    last = nc.vector.bn_aggr(z_mv[:, t], z_bst[:, t])
                last.then_inc(z_moments, 1)
                dve.wait_ge(z_moments, n)
                nc.vector.tensor_scalar(z_u[:, :], z_mv[:, :, 1], LN_EPS, RMS_EPS ** 2 / C, ALU.add, ALU.mult
                                        ).then_inc(z_u_set, 1)
                nc.vector.tensor_scalar(z_nm[:, :], z_mv[:, :, 0], -1.0, None, ALU.mult)
                dve.wait_ge(z_u_set, n)
                nc.vector.tensor_tensor(z_w[:, :], z_mv[:, :, 1], z_u[:, :], ALU.max).then_inc(z_w_set, 1)

            def zT_rest(b, n):
                dve.wait_ge(zT_hi, n)
                nc.vector.tensor_tensor(zT_all[:, b, LO], zT_ps, zT_all[:, b, HI].bitcast(F32), ALU.subtract
                                        ).then_inc(zT_lo, 1)

            def max_D(b, n):
                dve.wait_ge(LT_mm, n)
                freed(dve, D_exp, b)
                nc.vector.tensor_reduce(nmD[:, :], LT_ps, AX.X, ALU.max, negate=True).then_inc(D_max, 1)

            def max_C(b, n):
                dve.wait_ge(L_mm, n)
                freed(dve, C_exp, b)
                nc.vector.tensor_reduce(nmC[:, :], L_ps, AX.X, ALU.max, negate=True).then_inc(C_max, 1)

            def invert_ZD(b, n):
                dve.wait_ge(D_exp, n)
                freed(dve, Dn_ready, b)
                nc.vector.reciprocal(rZD[:, :], ZD[:, :]).then_inc(ZD_inv, 1)

            def CT_copy(b, n):
                dve.wait_ge(C_turned, n)
                nc.vector.tensor_copy(CT_all[:, b], CT_ps).then_inc(CT_ready, 1)
                nc.vector.reciprocal(rZC_all[:, b], ZC_all[:, b]).then_inc(ZC_inv, 1)

            def slots_rest(b, n):
                dve.wait_ge(slots_hi, n)
                nc.vector.scalar_tensor_tensor(out=slots_all[:, b, LO], in0=slots_ps, scalar=gx_col[:, 0:1],
                                               in1=slots_all[:, b, HI].bitcast(F32), op0=ALU.mult,
                                               op1=ALU.subtract).then_inc(slots_lo, 1)

            def h_rest(g):
                def stage(b, n):
                    dve.wait_ge(h_hi_ready, NG * b + g + 1)
                    freed(dve, PT_mm, NG * b + g - 1)
                    nc.vector.tensor_tensor(h_lo[:, g], h_f[:, g], h_hi[:, g].bitcast(F32), ALU.subtract
                                            ).then_inc(h_lo_ready, 1)
                return stage

            def PT_copy(b, n):
                dve.wait_ge(PT_mm, NG * b + NG)
                freed(dve, P_turned, b)
                nc.vector.tensor_copy(PT_sb[:, :], PT_ps).then_inc(PT_ready, 1)

            def finish(b, n):
                dve.wait_ge(out_mm, n)
                dve.wait_ge(ZC_inv, n)
                dve.wait_ge(x1_saved, 16 * n)
                freed(dve, out_stored, 16 * b)
                for t in range(NT):
                    last = nc.vector.scalar_tensor_tensor(out=out_sb[:, t], in0=out_ps[:, t],
                                                          scalar=rZC_all[:, b, t:t + 1], in1=x1_all[:, b, t],
                                                          op0=ALU.mult, op1=ALU.add)
                last.then_inc(out_ready, 1)

            def before_start():
                x_moments_of(0)
                x_bias(0)
                x_moments_of(1)
                split_W1()

            def before_0():
                x_bias(1)
                x_moments_of(2)
                dve.wait_ge(ld_rows, 48)

            def before_2():
                x_bias(2)
                x_moments_of(3)
                slot_mean_square()

            run(dve, [[(-1, mask_scores), (-2, residual), (-2, z_sums), (-2, z_variance), (-1, a_sums), (-3, zT_rest),
                       (1, xT_rest), (-1, a_centre), (0, v_bias)],
                      [(LATE - 1, mask_scores), (LATE - 2, residual), (LATE - 2, z_sums), (1, max_D),
                       (LATE - 2, z_variance), (LATE - 1, a_sums), (LATE - 3, zT_rest), (LATE - 1, a_centre),
                       (1, invert_ZD), (1, max_C), (0, CT_copy), (0, slots_rest)],
                      [(1, max_D), (1, max_C), (1, invert_ZD), (0, CT_copy), (0, slots_rest)],
                      [(FIRST, h_rest(0)), (0, slots_rest), (0, CT_copy), (FIRST, h_rest(1))],
                      [(1, h_rest(0)), (0, PT_copy), (1, h_rest(1)), (-1, finish)]],
                {(ATTN, -1): before_start, (ATTN, 0): before_0, 
                 (ATTN, 1): lambda: dve.wait_ge(mask_set, 3), (ATTN, 2): before_2,
                 (ATTN, 3): lambda: x_bias(3), (ATTN, 4): slot_normalise,
                 (ATTN, B - 1): slot_rest})

        @block.tensor
        def _(pe):
            def three_pass(dst, stationary, moving, start, stop):
                nc.tensor.matmul(dst, stationary(HI), moving(HI), start=start, stop=False)
                nc.tensor.matmul(dst, stationary(HI), moving(LO), start=False, stop=False)
                return nc.tensor.matmul(dst, stationary(LO), moving(HI), start=False, stop=stop)

            def turn_x(b, n):
                pe.wait_ge(xn_ready, n)
                freed(pe, xT_hi, b)
                freed(pe, xT_lo, b)
                for t in range(NT):
                    last = nc.tensor.transpose(xT_ps[:, t * P:(t + 1) * P], xn[:, t], ident[:, :])
                last.then_inc(x_turned, 1)

            def hidden(b, n):
                pe.wait_ge(xT_hi, n)
                pe.wait_ge(xT_lo, n)
                freed(pe, hid_ready, 3 * b)
                for m in range(3):
                    dst = hqk_ps[:, m] if m < 2 else hv_ps
                    last = three_pass(dst, lambda s: W1_s[:, m, s], lambda s: xT_s[:, s], True, True)
                    if m:
                        last.then_inc(hid_mm, 1)

            def project(b, n):
                if first_batch(b):
                    pe.wait_ge(ld_W2, 48)
                freed(pe, qk_ready, 2 * b)
                for m in range(2):
                    pe.wait_ge(hid_ready, 3 * b + m + 1)
                    last = nc.tensor.matmul(qk_ps[:, m], W2_sb[:, m], hidT[:, m], start=True, stop=True)
                last.then_inc(qk_mm, 1)
                pe.wait_ge(hid_ready, 3 * b + 3)
                freed(pe, v_ready, b)
                for t in range(NT):
                    last = nc.tensor.matmul(v_ps[:, t], hidT[:, 2, t * P:(t + 1) * P], W2_sb[:, 2],
                                            start=True, stop=True)
                last.then_inc(v_mm, 1)

            def scores(b, n):
                pe.wait_ge(qk_ready, 2 * b + 2)
                freed(pe, s_ready, b)
                nc.tensor.matmul(s_ps[:, 0:T], qkT[:, 1, 0:P], qkT[:, 0], start=True, stop=True)
                nc.tensor.matmul(s_ps[:, T:SW], qkT[:, 1, P:T], qkT[:, 0, P:T], start=True, stop=True
                                 ).then_inc(s_mm, 1)

            def attend(b, n):
                pe.wait_ge(s_ready, n)
                pe.wait_ge(v_ready, n)
                freed(pe, ac_ready, b)
                nc.tensor.matmul(a_ps[:, 0], sT[:, 0:P], v_sb[:, 0], start=True, stop=True)
                nc.tensor.matmul(a_ps[:, 1], sT[:, P:T], v_sb[:, 0], start=True, stop=False)
                nc.tensor.matmul(a_ps[:, 1], sT[:, T:SW], v_sb[:, 1], start=False, stop=True).then_inc(a_mm, 1)

            def turn_z(b, n):
                pe.wait_ge(z_ready, n)
                freed(pe, zT_hi, b)
                freed(pe, zT_lo, b)
                for t in range(NT):
                    last = nc.tensor.transpose(zT_ps[:, t * P:(t + 1) * P], z_cur[:, t], ident[:, :])
                last.then_inc(z_turned, 1)

            def turn_slots():
                pe.wait_ge(slot_n_set, 1)
                pe.wait_ge(xT_hi, B)
                pe.wait_ge(xT_lo, B)
                for e in range(NE):
                    last = nc.tensor.transpose(slotT_ps[:, e * P:(e + 1) * P], slot_n[:, e], ident[:, :])
                last.then_inc(slot_turned, 1)

            def logits_T(b, n):
                pe.wait_ge(zT_hi, n)
                pe.wait_ge(zT_lo, n)
                freed(pe, D_exp, b)
                if first_batch(b):
                    pe.wait_ge(slotT_lo, 1)
                    pe.wait_ge(hid_ready, 3 * B)
                    pe.wait_ge(qk_ready, 2 * B)
                    pe.wait_ge(v_ready, B)
                for e in range(NE):
                    last = three_pass(LT_ps[:, e], lambda s: slotT_s[:, s, e * P:(e + 1) * P],
                                      lambda s: zT_all[:, b, s], True, True)
                last.then_inc(LT_mm, 1)

            def logits(b, n):
                pe.wait_ge(zT_staged, 16 * n)
                freed(pe, C_exp, b)
                for t in range(NT):
                    last = three_pass(L_ps[:, t], lambda s: zT_st[:, s, t * P:(t + 1) * P],
                                      lambda s: slotT_s[:, s], True, True)
                last.then_inc(L_mm, 1)

            def turn_D(b, n):
                pe.wait_ge(Dn_ready, n)
                freed(pe, CT_ready, b)
                if first_batch(b):
                    pe.wait_ge(s_ready, B)
                    pe.wait_ge(ac_ready, B)
                for t in range(NT):
                    for e in range(NE):
                        last = nc.tensor.transpose(D_ps[:, t, e * P:(e + 1) * P], Dn[:, e, t * P:(t + 1) * P],
                                                   ident[:, :])
                last.then_inc(D_turned, 1)

            def turn_C(b, n):
                pe.wait_ge(C_exp, n)
                pe.wait_ge(D_ready, n)
                for e in range(NE):
                    for t in range(NT):
                        last = nc.tensor.transpose(CT_ps[:, e, t * P:(t + 1) * P], Cx[:, t, e * P:(e + 1) * P],
                                                   ident[:, :])
                last.then_inc(C_turned, 1)

            def slots(b, n):
                pe.wait_ge(D_ready, n)
                pe.wait_ge(z_staged, 16 * n)
                freed(pe, slots_lo, b)
                for t in range(NT):
                    last = nc.tensor.matmul(slots_ps, z_st[:, t], D_sb[:, t], start=(t == 0), stop=(t == NT - 1))
                last.then_inc(slots_mm, 1)

            def expert_hidden(g):
                def stage(b, n):
                    pe.wait_ge(slots_hi, n)
                    pe.wait_ge(slots_lo, n)
                    freed(pe, h_ready, NG * b + g - 1)
                    if first_batch(b):
                        pe.wait_ge(w_lo, 2)
                        pe.wait_ge((D_exp, C_exp)[g], B)
                    for j in range(GH):
                        m = g * GH + j
                        last = three_pass(h_ps[g][:, j], lambda s: w1_s[:, s, m * P:(m + 1) * P],
                                          lambda s: slots_all[:, b, s], True, True)
                    last.then_inc(h_mm, 1)
                return stage

            def expert_out(g):
                def stage(b, n):
                    pe.wait_ge(h_hi_ready, NG * b + g + 1)
                    pe.wait_ge(h_lo_ready, NG * b + g + 1)
                    if g == 0:
                        freed(pe, PT_ready, b)
                        if first_batch(b):
                            pe.wait_ge(zT_lo, B)
                    for j in range(GH):
                        m = g * GH + j
                        last = three_pass(PT_ps, lambda s: w2_s[:, s, m],
                                          lambda s: (h_hi, h_lo)[s][:, g, j], m == 0, m == NH - 1)
                    last.then_inc(PT_mm, 1)
                return stage

            def turn_P(b, n):
                pe.wait_ge(PT_ready, n)
                freed(pe, P_ready, b)
                if first_batch(b):
                    pe.wait_ge(CT_ready, B)
                for e in range(NE):
                    last = nc.tensor.transpose(P_ps[:, e], PT_sb[:, e * P:(e + 1) * P], ident[:, :])
                last.then_inc(P_turned, 1)

            def combine(b, n):
                pe.wait_ge(P_ready, n)
                CT = CT_st
                if last_batch(b):
                    CT = CT_all[:, b]
                else:
                    pe.wait_ge(CT_staged, 16 * n)
                freed(pe, out_ready, b)
                for t in range(NT):
                    for e in range(NE):
                        last = nc.tensor.matmul(out_ps[:, t], CT[:, e, t * P:(t + 1) * P], P_sb[:, e],
                                                start=(e == 0), stop=(e == NE - 1))
                last.then_inc(out_mm, 1)

            def weights_in():
                pe.wait_ge(W1_split, 2)

            run(pe, [[(-1, scores), (0, hidden), (-3, turn_z), (-1, attend), (1, turn_x), (0, project)],
                     [(LATE - 1, scores), (LATE - 3, turn_z), (1, logits_T), (LATE - 1, attend), (0, turn_D),
                      (1, logits), (0, slots), (0, turn_C)],
                     [(1, logits_T), (0, turn_D), (1, logits), (0, slots), (0, turn_C)],
                     [(FIRST, expert_hidden(0)), (0, turn_D), (FIRST, expert_hidden(1)), (0, slots), (0, turn_C)],
                     [(1, expert_hidden(0)), (0, expert_out(0)), (1, expert_hidden(1)), (0, expert_out(1)),
                      (-1, combine), (0, turn_P)]],
                {(ATTN, -1): lambda: pe.wait_ge(ident_set, 2), (ATTN, 0): weights_in,
                 (ATTN, B - 1): turn_slots})


_INS = ['L0_attn_x', 'L0_attn_W1q', 'L0_attn_b1q', 'L0_attn_W2q', 'L0_attn_b2q', 'L0_attn_W1k', 'L0_attn_b1k',
        'L0_attn_W2k', 'L0_attn_b2k', 'L0_attn_W1v', 'L0_attn_b1v', 'L0_attn_W2v', 'L0_attn_b2v', 'L0_attn_ln_w',
        'L0_attn_ln_b', 'L0_ffn_gamma_x', 'L0_ffn_gamma_slot', 'L0_ffn_slot_embeds', 'L0_ffn_w1', 'L0_ffn_w2']
_OUTS = [((8, 256, 128), 'float32')]


def kernel(**inputs):
    import numpy as _np
    import concourse.bacc as _bacc
    from concourse import mybir as _mybir
    from concourse.bass_utils import run_bass_kernel_spmd as _run

    nc = _bacc.Bacc("TRN2", target_bir_lowering=False, num_devices=1)
    arrays, args = {}, []
    for name in _INS:
        a = _np.ascontiguousarray(inputs[name])
        arrays[f"in_{name}_dram"] = a
        args.append(nc.dram_tensor(f"in_{name}_dram", a.shape, _mybir.dt.from_np(a.dtype), kind="ExternalInput").ap())
    for i, (shape, dtype) in enumerate(_OUTS):
        dt = _mybir.dt.from_np(_np.dtype(dtype))
        args.append(nc.dram_tensor(f"out_{i}_dram", shape, dt, kind="ExternalOutput").ap())
    build(nc, *args)
    r = _run(nc, [arrays], core_ids=[0])
    got = tuple(r.results[0][f"out_{i}_dram"] for i in range(len(_OUTS)))
    return got[0]
```

```python
from contextlib import ExitStack

import concourse.bass as bass
from concourse import mybir

F32 = mybir.dt.float32
F32R = mybir.dt.float32r
ALU = mybir.AluOpType
ACT = mybir.ActivationFunctionType
AX = mybir.AxisListType

LN_EPS = 1e-5
RMS_EPS = 1e-12
HI, LO = 0, 1
ATTN, INTO_ROUTE, ROUTE, INTO_EXPERT, EXPERT = range(5)


def build(nc, x, W1q, b1q, W2q, b2q, W1k, b1k, W2k, b2k, W1v, b1v, W2v, b2v, ln_w, ln_b,
          gamma_x, gamma_slot, slot_embeds, w1, w2, out):
    B, T, C = x.shape
    P = 128
    NT = T // P
    E = slot_embeds.shape[0] * slot_embeds.shape[1]
    NE = E // P
    HID = w1.shape[1]
    NH = HID // P
    NG = 2
    GH = NH // NG
    assert C == P and NT == 2 and NE == 4 and NH == 4
    inv_scale = 1.0 / float((C * T) ** 0.5)
    SW = T + P
    X_GROUPS = [(0, 1), (1, 3), (3, 5), (5, B)]

    x_v = x.rearrange("b (t p) c -> p b t c", p=P)
    out_v = out.rearrange("b (t p) c -> p b t c", p=P)

    ctx = ExitStack()
    with ctx:
        def sb(name, shape, dt=F32):
            return ctx.enter_context(nc.sbuf_tensor(name, [P] + list(shape), dt))

        def sem(name):
            return ctx.enter_context(nc.semaphore(name))

        x_sb = sb("x_sb", [B, NT, C])
        W1_sb = sb("W1_sb", [3, C])
        W2_sb = sb("W2_sb", [3, C])
        b1_col = sb("b1_col", [3])
        b2_col = sb("b2_col", [2])
        b2v_row = sb("b2v_row", [C])
        lnw_row = sb("lnw_row", [C])
        lnb_row = sb("lnb_row", [C])
        gx_col = sb("gx_col", [1])
        gs_col = sb("gs_col", [1])
        gg_col = sb("gg_col", [1])
        slot_raw = sb("slot_raw", [NE, C])
        slot_sq = sb("slot_sq", [NE, C])
        slot_n = sb("slot_n", [NE, C])
        slot_ss = sb("slot_ss", [NE])
        slot_ms = sb("slot_ms", [NE])
        slot_r = sb("slot_r", [NE])
        slotT_s = sb("slotT_s", [2, E], F32R)
        w1_raw = sb("w1_raw", [HID])
        w1_s = sb("w1_s", [2, HID], F32R)
        w2_raw = sb("w2_raw", [NH, C])
        w2_s = sb("w2_s", [2, NH, C], F32R)
        ident = sb("ident", [P])
        mask = sb("mask", [SW])
        minus_half = sb("minus_half", [B * NT])
        gelu_warm = sb("gelu_warm", [1])

        x_bst = sb("x_bst", [B, NT, 6])
        x_mv = sb("x_mv", [B, NT, 2])
        x_ve = sb("x_ve", [B * NT])
        x_rs = sb("x_rs", [B * NT])
        x_nb = sb("x_nb", [B * NT])
        xn = sb("xn", [NT, C])
        xT = sb("xT", [T])
        hidT = sb("hidT", [3, T])
        qkT = sb("qkT", [2, T])
        v_sb = sb("v_sb", [NT, C])
        sT = sb("sT", [SW])
        a_bst = sb("a_bst", [NT, 6])
        a_mv = sb("a_mv", [NT, 2])
        a_ve = sb("a_ve", [NT])
        a_rs = sb("a_rs", [NT])
        ac = sb("ac", [NT, C])
        xb = sb("xb", [NT, C])
        x1_cur = sb("x1_cur", [NT, C])
        z_bst = sb("z_bst", [NT, 6])
        z_mv = sb("z_mv", [NT, 2])
        z_nm = sb("z_nm", [NT])
        z_u = sb("z_u", [NT])
        z_w = sb("z_w", [NT])
        z_rs = sb("z_rs", [NT])
        z_cur = sb("z_cur", [NT, C])

        x1_all = sb("x1_all", [B, NT, C])
        z_all = sb("z_all", [B, NT, C])
        zT_all = sb("zT_all", [B, 2, T], F32R)
        slots_all = sb("slots_all", [B, 2, E], F32R)
        CT_all = sb("CT_all", [B, NE, T])
        ZC_all = sb("ZC_all", [B, NT])
        rZC_all = sb("rZC_all", [B, NT])

        z_st = sb("z_st", [2, NT, C], F32R)
        zT_st = sb("zT_st", [2, T], F32R)
        nmC = sb("nmC", [NT])
        nmD = sb("nmD", [NE])
        ZD = sb("ZD", [NE])
        rZD = sb("rZD", [NE])
        Cx = sb("Cx", [NT, E])
        Dx = sb("Dx", [NE, T])
        Dn = sb("Dn", [NE, T])
        D_sb = sb("D_sb", [2, NT, E], F32R)

        CT_st = sb("CT_st", [NE, T])
        h_f = sb("h_f", [NG, GH, E])
        h_hi = sb("h_hi", [NG, GH, E], F32R)
        h_lo = sb("h_lo", [NG, GH, E], F32R)
        PT_sb = sb("PT_sb", [E])
        P_sb = sb("P_sb", [NE, C])
        out_sb = sb("out_sb", [NT, C])

        ps = ctx.enter_context(nc.psum_tensor("ps", [P, 8, 512], F32))
        xT_ps = ps[:, 0, 0:T]
        hqk_ps = ps[:, 1, :].rearrange("p (m t) -> p m t", m=2)
        hv_ps = ps[:, 2, 0:T]
        qk_ps = ps[:, 3, :].rearrange("p (m t) -> p m t", m=2)
        v_ps = ps[:, 4, 0:NT * C].rearrange("p (t c) -> p t c", t=NT)
        s_ps = ps[:, 5, 0:SW]
        a_ps = ps[:, 6, 0:NT * C].rearrange("p (t c) -> p t c", t=NT)
        zT_ps = ps[:, 7, 0:T]
        slotT_ps = ps[:, 0, :]
        L_ps = ps[:, 1:3, :]
        LT_ps = ps[:, 3:5, :].rearrange("p k (e t) -> p (k e) t", e=2)
        D_ps = ps[:, 5:7, :]
        CT_banks = [ps[:, k, :].rearrange("p (e t) -> p e t", e=2) for k in (5, 7, 6)]
        slots_ps = ps[:, 0, :]
        h_ps = [ps[:, 3:5, :], ps[:, 1:3, :]]
        PT_ps = ps[:, 6, :]
        P_ps = ps[:, 5, :].rearrange("p (e c) -> p e c", e=NE)
        out_ps = ps[:, 7, 0:NT * C].rearrange("p (t c) -> p t c", t=NT)

        ld_x = [sem(f"ld_x{g}") for g in range(len(X_GROUPS))]
        ld_W1, ld_W2, ld_b1, ld_b2, ld_rows, ld_slot, ld_w = (
            sem("ld_W1"), sem("ld_W2"), sem("ld_b1"), sem("ld_b2"), sem("ld_rows"), sem("ld_slot"),
            sem("ld_w"))
        ident_set, mask_set, half_set, gelu_warmed = (
            sem("ident_set"), sem("mask_set"), sem("half_set"), sem("gelu_warmed"))
        w_hi, w_lo, gg_set = sem("w_hi"), sem("w_lo"), sem("gg_set")
        slot_sq_done, slot_ms_set, slot_r_set, slot_n_set = (
            sem("slot_sq_done"), sem("slot_ms_set"), sem("slot_r_set"), sem("slot_n_set"))
        slot_turned, slotT_hi, slotT_lo = sem("slot_turned"), sem("slotT_hi"), sem("slotT_lo")

        x_stats, x_moments, x_eps, x_rstd, x_nb_set = (
            sem("x_stats"), sem("x_moments"), sem("x_eps"), sem("x_rstd"), sem("x_nb_set"))
        xn_ready, x_turned, xT_ready = sem("xn_ready"), sem("x_turned"), sem("xT_ready")
        hid_mm, hid_ready = sem("hid_mm"), sem("hid_ready")
        qk_mm, qk_ready, v_mm, v_ready = sem("qk_mm"), sem("qk_ready"), sem("v_mm"), sem("v_ready")
        s_mm, s_ready, a_mm = sem("s_mm"), sem("s_ready"), sem("a_mm")
        a_stats, a_moments, a_eps, a_rstd, ac_ready = (
            sem("a_stats"), sem("a_moments"), sem("a_eps"), sem("a_rstd"), sem("ac_ready"))
        xb_ready, x1_ready = sem("xb_ready"), sem("x1_ready")
        z_stats, z_moments, z_u_set, z_w_set, z_rstd, z_ready = (
            sem("z_stats"), sem("z_moments"), sem("z_u_set"), sem("z_w_set"), sem("z_rstd"), sem("z_ready"))
        x1_saved, z_saved = sem("x1_saved"), sem("z_saved")
        z_turned, zT_hi, zT_lo = sem("z_turned"), sem("zT_hi"), sem("zT_lo")

        zT_staged = sem("zT_staged")
        z_hi, z_lo = sem("z_hi"), sem("z_lo")
        LT_mm, L_mm, D_max, C_max = sem("LT_mm"), sem("L_mm"), sem("D_max"), sem("C_max")
        ZD_inv = [sem("ZD_inv0"), sem("ZD_inv1")]
        D_exp_half, D_exp, C_exp, ZC_inv, Dn_ready = (
            sem("D_exp_half"), sem("D_exp"), sem("C_exp"), sem("ZC_inv"), sem("Dn_ready"))
        D_turned, D_hi, D_lo = sem("D_turned"), sem("D_hi"), sem("D_lo")
        C_turned = [sem("C_turned0"), sem("C_turned1")]
        CT_ready = [sem("CT_ready0"), sem("CT_ready1")]
        slots_mm, slots_hi, slots_lo = sem("slots_mm"), sem("slots_hi"), sem("slots_lo")

        CT_staged = sem("CT_staged")
        h_mm, h_ready, h_hi_ready, h_lo_ready, PT_mm = (
            sem("h_mm"), sem("h_ready"), sem("h_hi_ready"), sem("h_lo_ready"), sem("PT_mm"))
        PT_ready, P_turned, P_ready, out_mm, out_ready = (
            sem("PT_ready"), sem("P_turned"), sem("P_ready"), sem("out_mm"), sem("out_ready"))
        out_stored = sem("out_stored")

        block = ctx.enter_context(nc.Block())

        SCHEDULE = [(ATTN, -1, 4), (ATTN, 4, B - 1), (ATTN, B - 1, B), (INTO_ROUTE, -1, 2), (ROUTE, 2, B - 2),
                    (ROUTE, B - 2, B - 1), (INTO_EXPERT, B - 1, B), (EXPERT, 0, 2), (EXPERT, 2, B - 1),
                    (EXPERT, B - 1, B + 1)]
        LOOPS = [(ATTN, 4, B - 1), (ROUTE, 2, B - 2), (EXPERT, 2, B - 1)]
        LATE = B + 1
        FIRST = 1 - B

        def run(eng, phases, before):
            for part in SCHEDULE:
                phase, k0, k1 = part
                stages = phases[phase]
                if part in LOOPS:
                    before.get((phase, k0), lambda: None)()
                    if not stages:
                        continue
                    offsets = [o for o, _ in stages]
                    with eng.Fori(k0, k1) as k:
                        at = {o: in_register(eng, k + o, k0 + o, k1 - 1 + o)
                              for o in range(min(offsets), max(offsets) + 2)}
                        for o, stage in stages:
                            stage(at[o], at[o + 1])
                else:
                    for k in range(k0, k1):
                        before.get((phase, k), lambda: None)()
                        for o, stage in stages:
                            if 0 <= k + o < B:
                                stage(k + o, k + o + 1)

        def in_register(eng, value, least, most):
            return eng.snap(eng.to_reg(value), min_val=least, max_val=most)

        def first_batch(b):
            return isinstance(b, int) and b == 0

        def CT_ps(b, h):
            return CT_banks[2 if h == 1 and first_batch(b) else h]

        def last_batch(b):
            return isinstance(b, int) and b == B - 1

        def freed(eng, semaphore, count):
            if not (isinstance(count, int) and count <= 0):
                eng.wait_ge(semaphore, count)

        def own_instruction(eng):
            eng.wait_ge(half_set, 1)

        @block.sync
        def _(sp):
            sp.dma_start(x_sb[:, 0], x_v[:, 0]).then_inc(ld_x[0], 16)
            for m, W in enumerate((W1q, W1k, W1v)):
                sp.dma_start(W1_sb[:, m], W).then_inc(ld_W1, 16)
            sp.dma_start(x_sb[:, 1:3], x_v[:, 1:3]).then_inc(ld_x[1], 16)
            for m, b in enumerate((b1q, b1k, b1v)):
                sp.dma_start(b1_col[:, m:m + 1], b[:, None]).then_inc(ld_b1, 16)
            sp.dma_start(x_sb[:, 3:5], x_v[:, 3:5]).then_inc(ld_x[2], 16)
            for m, W in enumerate((W2q, W2k, W2v)):
                sp.dma_start(W2_sb[:, m], W).then_inc(ld_W2, 16)
            for m, b in enumerate((b2q, b2k)):
                sp.dma_start(b2_col[:, m:m + 1], b[:, None]).then_inc(ld_b2, 16)
            sp.dma_start(x_sb[:, 5:B], x_v[:, 5:B]).then_inc(ld_x[3], 16)
            sp.dma_start(w1_raw[:, :], w1).then_inc(ld_w, 16)
            sp.dma_start(w2_raw[:, :, :], w2.rearrange("(k p) c -> p k c", p=P)).then_inc(ld_w, 16)

            def save_x1(b, n):
                own_instruction(sp)
                sp.wait_ge(x1_ready, n)
                sp.dma_start(x1_all[:, b], x1_cur[:, :, :]).then_inc(x1_saved, 16)

            def save_z(b, n):
                own_instruction(sp)
                sp.wait_ge(z_ready, n)
                sp.dma_start(z_all[:, b], z_cur[:, :, :]).then_inc(z_saved, 16)

            def stage_zT(b, n):
                own_instruction(sp)
                sp.wait_ge(zT_hi, n)
                sp.wait_ge(zT_lo, n)
                freed(sp, L_mm, b)
                sp.dma_start(zT_st[:, :, :].bitcast(F32), zT_all[:, b].bitcast(F32)).then_inc(zT_staged, 16)

            def stage_CT(b, n):
                if last_batch(b):
                    return
                own_instruction(sp)
                sp.wait_ge(CT_ready[0], n)
                sp.wait_ge(CT_ready[1], n)
                freed(sp, out_mm, b)
                sp.dma_start(CT_st[:, :, :], CT_all[:, b]).then_inc(CT_staged, 16)

            def store(b, n):
                own_instruction(sp)
                sp.wait_ge(out_ready, n)
                sp.dma_start(out_v[:, b], out_sb[:, :, :]).then_inc(out_stored, 16)

            run(sp, [[(-2, save_x1), (-2, save_z)],
                     [(LATE - 2, save_x1), (2, stage_zT), (LATE - 2, save_z)],
                     [(2, stage_zT)],
                     [],
                     [(0, stage_CT), (-1, store)]],
                {(ATTN, B - 1): lambda: stage_zT(0, 1)})
            sp.wait_ge(out_stored, 16 * B)

        @block.gpsimd
        def _(pool):
            nc.gpsimd.memset(minus_half[:, :], -0.5).then_inc(half_set, 1)
            nc.gpsimd.memset(ident[:, :], 0.0).then_inc(ident_set, 1)
            nc.gpsimd.memset(mask[:, :], inv_scale).then_inc(mask_set, 1)
            pool.wait_ge(ident_set, 1)
            nc.gpsimd.affine_select(out=ident[:, :], in_=ident[:, :], compare_op=ALU.not_equal, fill=1.0,
                                    base=0, pattern=[[-1, P]], channel_multiplier=1).then_inc(ident_set, 1)
            for row, b in ((b2v_row, b2v), (lnw_row, ln_w)):
                pool.dma_start(row[:, :], b.partition_broadcast(P)).then_inc(ld_rows, 16)

            def load_slots():
                pool.dma_start(slot_raw[:, :, :],
                               slot_embeds.rearrange("e t c -> (e t) c").rearrange("(k p) c -> p k c", p=P)
                               ).then_inc(ld_slot, 16)
                pool.dma_start(gx_col[:, :], gamma_x[:, None]).then_inc(ld_slot, 16)
                pool.dma_start(gs_col[:, :], gamma_slot[:, None]).then_inc(ld_slot, 16)

            def mask_triangles():
                pool.wait_ge(mask_set, 1)
                for c0 in (0, T):
                    tri = mask[:, c0:c0 + P]
                    nc.gpsimd.affine_select(out=tri, in_=tri, compare_op=ALU.is_ge, fill=0.0, base=0,
                                            pattern=[[1, P]], channel_multiplier=-1).then_inc(mask_set, 1)

            def x_rsqrt(g):
                b0, b1 = X_GROUPS[g]
                cols = slice(b0 * NT, b1 * NT)
                pool.wait_ge(half_set, 1)
                pool.wait_ge(x_moments, g + 1)
                nc.gpsimd.tensor_scalar(x_ve[:, cols], x_mv[:, b0:b1, :, 1].rearrange("p b t -> p (b t)"),
                                        LN_EPS, 1.0, ALU.add, ALU.mult).then_inc(x_eps, 1)
                pool.wait_ge(x_eps, g + 1)
                nc.gpsimd.tensor_tensor(x_rs[:, cols], x_ve[:, cols], minus_half[:, 0:(b1 - b0) * NT], ALU.pow
                                        ).then_inc(x_rstd, 1)

            def slot_rsqrt():
                pool.wait_ge(slot_ms_set, 1)
                nc.gpsimd.tensor_tensor(slot_r[:, :], slot_ms[:, :], minus_half[:, 0:NE], ALU.pow
                                        ).then_inc(slot_r_set, 1)

            def experts_rest(i, w_s, w_raw):
                pool.wait_ge(w_hi, i + 1)
                nc.gpsimd.tensor_tensor(w_s[:, LO], w_raw, w_s[:, HI].bitcast(F32), ALU.subtract).then_inc(w_lo, 1)

            def x_plus_bias(b, n):
                freed(pool, x1_ready, b)
                nc.gpsimd.tensor_tensor(xb[:, :, :], x_sb[:, b],
                                        lnb_row[:, :].unsqueeze(1).to_broadcast([P, NT, C]), ALU.add
                                        ).then_inc(xb_ready, 1)

            def a_rsqrt(b, n):
                pool.wait_ge(a_eps, n)
                freed(pool, x1_ready, b)
                nc.gpsimd.tensor_tensor(a_rs[:, :], a_ve[:, :], minus_half[:, 0:NT], ALU.pow).then_inc(a_rstd, 1)

            def z_rsqrt(b, n):
                pool.wait_ge(z_w_set, n)
                nc.gpsimd.tensor_tensor(z_rs[:, :], z_w[:, :], minus_half[:, 0:NT], ALU.pow).then_inc(z_rstd, 1)

            def z_normalise(b, n):
                landed = 16 * b if isinstance(b, int) else in_register(pool, 16 * b, 16, 16 * B)
                own_instruction(pool)
                pool.wait_ge(z_rstd, n)
                freed(pool, z_turned, b)
                freed(pool, z_saved, landed)
                for t in range(NT):
                    last = nc.gpsimd.tensor_scalar(z_cur[:, t], x1_cur[:, t], z_nm[:, t:t + 1], z_rs[:, t:t + 1],
                                                   ALU.add, ALU.mult)
                last.then_inc(z_ready, 1)

            def D_normalise(b, n):
                own_instruction(pool)
                freed(pool, D_turned, b)
                for e in range(NE):
                    if e % 2 == 0:
                        if e > 0:
                            own_instruction(pool)
                        pool.wait_ge(ZD_inv[e // 2], n)
                    last = nc.gpsimd.tensor_scalar(Dn[:, e], Dx[:, e], rZD[:, e:e + 1], 1.0, ALU.mult, ALU.mult)
                last.then_inc(Dn_ready, 1)

            def z_split(b, n):
                landed = 16 * n if isinstance(n, int) else in_register(pool, 16 * n, 16, 16 * B)
                own_instruction(pool)
                pool.wait_ge(z_saved, landed)
                freed(pool, slots_mm, b)
                nc.gpsimd.tensor_copy(z_st[:, HI], z_all[:, b]).then_inc(z_hi, 1)
                own_instruction(pool)
                pool.wait_ge(z_hi, n)
                nc.gpsimd.tensor_tensor(z_st[:, LO], z_all[:, b], z_st[:, HI].bitcast(F32), ALU.subtract
                                        ).then_inc(z_lo, 1)

            def before_start():
                x_rsqrt(0)
                pool.dma_start(lnb_row[:, :], ln_b.partition_broadcast(P)).then_inc(ld_rows, 16)

            def before_0():
                x_rsqrt(1)
                mask_triangles()

            def before_1():
                pool.wait_ge(ld_rows, 48)
                load_slots()
                x_rsqrt(2)

            def before_2():
                experts_rest(0, w1_s, w1_raw[:, :])
                x_rsqrt(3)

            run(pool, [[(-1, x_plus_bias), (-2, z_rsqrt), (-2, z_normalise), (-1, a_rsqrt)],
                       [(0, z_split), (LATE - 1, x_plus_bias), (LATE - 2, z_rsqrt), (LATE - 2, z_normalise),
                        (LATE - 1, a_rsqrt), (1, D_normalise)],
                       [(0, z_split), (1, D_normalise)], [(0, z_split)], []],
                {(ATTN, -1): before_start, (ATTN, 0): before_0, (ATTN, 1): before_1, (ATTN, 2): before_2,
                 (ATTN, 3): slot_rsqrt, (ATTN, B - 1): lambda: experts_rest(1, w2_s, w2_raw[:, :, :])})

        @block.scalar
        def _(act):
            act.wait_ge(half_set, 1)
            nc.scalar.activation(gelu_warm[:, :], minus_half[:, 0:1], ACT.Gelu).then_inc(gelu_warmed, 1)

            def x_group(g):
                act.wait_ge(ld_x[g], 16)
                act.wait_ge(x_rstd, g + 1)
                act.wait_ge(x_nb_set, g + 1)

            def x_normalise(b, n):
                freed(act, x_turned, b)
                for t in range(NT):
                    last = nc.scalar.activation(xn[:, t], x_sb[:, b, t], ACT.Identity,
                                                bias=x_nb[:, bass.ds(b * NT + t, 1)],
                                                scale=x_rs[:, bass.ds(b * NT + t, 1)])
                last.then_inc(xn_ready, 1)

            def hidden_qk(b, n):
                freed(act, v_mm, b)
                act.wait_ge(hid_mm, 2 * b + 1)
                for m in range(2):
                    nc.scalar.activation(hidT[:, m], hqk_ps[:, m], ACT.Gelu, bias=b1_col[:, m:m + 1]
                                         ).then_inc(hid_ready, 1)

            def hidden_v(b, n):
                act.wait_ge(hid_mm, 2 * b + 2)
                nc.scalar.activation(hidT[:, 2], hv_ps, ACT.Gelu, bias=b1_col[:, 2:3]).then_inc(hid_ready, 1)

            def xT_copy(b, n):
                act.wait_ge(x_turned, n)
                freed(act, hid_mm, 2 * b)
                nc.scalar.copy(xT[:, :], xT_ps).then_inc(xT_ready, 1)

            def qk(b, n):
                act.wait_ge(qk_mm, n)
                freed(act, s_mm, b)
                for m in range(2):
                    nc.scalar.activation(qkT[:, m], qk_ps[:, m], ACT.Identity, bias=b2_col[:, m:m + 1]
                                         ).then_inc(qk_ready, 1)

            def zT_round(b, n):
                act.wait_ge(z_turned, n)
                nc.scalar.copy(zT_all[:, b, HI], zT_ps).then_inc(zT_hi, 1)

            def round_experts():
                act.wait_ge(ld_w, 32)
                nc.scalar.copy(w1_s[:, HI], w1_raw[:, :]).then_inc(w_hi, 1)
                nc.scalar.copy(w2_s[:, HI], w2_raw[:, :, :]).then_inc(w_hi, 1)

            def slot_squares():
                act.wait_ge(ld_slot, 48)
                for e in range(NE):
                    nc.scalar.activation(slot_sq[:, e], slot_raw[:, e], ACT.Square,
                                         accum_out=slot_ss[:, e:e + 1]).then_inc(slot_sq_done, 1)

            def slot_round():
                act.wait_ge(slot_turned, 1)
                act.wait_ge(gg_set, 1)
                nc.scalar.activation(slotT_s[:, HI], slotT_ps, ACT.Identity, scale=gg_col[:, 0:1]
                                     ).then_inc(slotT_hi, 1)

            def D_back(b, n):
                act.wait_ge(D_turned, n)
                freed(act, slots_mm, b)
                nc.scalar.copy(D_sb[:, HI], D_ps).then_inc(D_hi, 1)

            def CT_copy1(b, n):
                act.wait_ge(C_turned[1], n)
                nc.scalar.copy(CT_all[:, b, 2:4], CT_ps(b, 1)).then_inc(CT_ready[1], 1)

            def exp_D(b, n):
                act.wait_ge(D_max, n)
                freed(act, Dn_ready, b)
                freed(act, ZD_inv[1], b)
                for e in range(NE):
                    last = nc.scalar.activation(Dx[:, e], LT_ps[:, e], ACT.Exp, bias=nmD[:, e:e + 1],
                                                accum_out=ZD[:, e:e + 1])
                    if e % 2 == 1:
                        last.then_inc((D_exp_half, D_exp)[e // 2], 1)

            def slots_round(b, n):
                act.wait_ge(slots_mm, n)
                nc.scalar.activation(slots_all[:, b, HI], slots_ps, ACT.Identity, scale=gx_col[:, 0:1]
                                     ).then_inc(slots_hi, 1)

            def exp_C(b, n):
                act.wait_ge(C_max, n)
                freed(act, C_turned[0], b)
                for t in range(NT):
                    last = nc.scalar.activation(Cx[:, t], L_ps[:, t], ACT.Exp, bias=nmC[:, t:t + 1],
                                                accum_out=ZC_all[:, b, t:t + 1])
                last.then_inc(C_exp, 1)

            def gelu_group(g):
                def stage(b, n):
                    act.wait_ge(h_mm, NG * b + g + 1)
                    freed(act, h_lo_ready, NG * b + g - 1)
                    nc.scalar.activation(h_f[:, g], h_ps[g], ACT.Gelu).then_inc(h_ready, 1)
                    act.wait_ge(h_ready, NG * b + g + 1)
                    freed(act, PT_mm, NG * b + g - 1)
                    nc.scalar.copy(h_hi[:, g], h_f[:, g]).then_inc(h_hi_ready, 1)
                return stage

            def P_copy(b, n):
                act.wait_ge(P_turned, n)
                freed(act, out_mm, b)
                nc.scalar.copy(P_sb[:, :, :], P_ps).then_inc(P_ready, 1)

            def before_0():
                x_group(1)
                act.wait_ge(ld_b1, 48)
                act.wait_ge(ld_b2, 32)

            def before_2():
                slot_squares()
                x_group(2)

            def fetch_gelu():
                nc.scalar.activation(gelu_warm[:, :], minus_half[:, 0:1], ACT.Gelu).then_inc(gelu_warmed, 1)

            run(act, [[(1, x_normalise), (0, hidden_qk), (0, hidden_v), (-3, zT_round), (1, xT_copy), (0, qk)],
                      [(LATE - 3, zT_round), (0, D_back), (1, exp_D), (0, CT_copy1), (0, slots_round), (1, exp_C)],
                      [(0, D_back), (1, exp_D), (0, CT_copy1), (0, slots_round), (1, exp_C)],
                      [(0, D_back), (FIRST, gelu_group(0)), (0, CT_copy1), (0, slots_round), (FIRST, gelu_group(1))],
                      [(1, gelu_group(0)), (1, gelu_group(1)), (0, P_copy)]],
                {(ATTN, -1): lambda: x_group(0), (ATTN, 0): before_0, (ATTN, 1): round_experts, (ATTN, 2): before_2,
                 (ATTN, 4): lambda: x_group(3), (ATTN, B - 1): slot_round, (INTO_EXPERT, B - 1): fetch_gelu})

        @block.vector
        def _(dve):
            def x_moments_of(g):
                b0, b1 = X_GROUPS[g]
                dve.wait_ge(ld_x[g], 16)
                for b in range(b0, b1):
                    for t in range(NT):
                        last = nc.vector.bn_stats(x_bst[:, b, t], x_sb[:, b, t])
                last.then_inc(x_stats, 1)
                dve.wait_ge(x_stats, g + 1)
                for b in range(b0, b1):
                    for t in range(NT):
                        last = nc.vector.bn_aggr(x_mv[:, b, t], x_bst[:, b, t])
                last.then_inc(x_moments, 1)

            def x_bias(g):
                b0, b1 = X_GROUPS[g]
                cols = slice(b0 * NT, b1 * NT)
                dve.wait_ge(x_moments, g + 1)
                dve.wait_ge(x_rstd, g + 1)
                nc.vector.scalar_tensor_tensor(out=x_nb[:, cols],
                                               in0=x_mv[:, b0:b1, :, 0].rearrange("p b t -> p (b t)"), scalar=-1.0,
                                               in1=x_rs[:, cols], op0=ALU.mult, op1=ALU.mult).then_inc(x_nb_set, 1)

            def slot_mean_square():
                dve.wait_ge(slot_sq_done, NE)
                nc.vector.tensor_scalar(slot_ms[:, :], slot_ss[:, :], 1.0 / C, RMS_EPS ** 2 / C,
                                        ALU.mult, ALU.max).then_inc(slot_ms_set, 1)
                dve.wait_ge(ld_slot, 48)
                nc.vector.tensor_tensor(gg_col[:, :], gx_col[:, :], gs_col[:, :], ALU.mult).then_inc(gg_set, 1)

            def slot_normalise():
                dve.wait_ge(slot_r_set, 1)
                for e in range(NE):
                    last = nc.vector.tensor_scalar(slot_n[:, e], slot_raw[:, e], slot_r[:, e:e + 1], None, ALU.mult)
                last.then_inc(slot_n_set, 1)

            def slot_rest():
                dve.wait_ge(slotT_hi, 1)
                nc.vector.scalar_tensor_tensor(out=slotT_s[:, LO], in0=slotT_ps, scalar=gg_col[:, 0:1],
                                               in1=slotT_s[:, HI].bitcast(F32), op0=ALU.mult, op1=ALU.subtract
                                               ).then_inc(slotT_lo, 1)

            def v_bias(b, n):
                dve.wait_ge(v_mm, n)
                freed(dve, a_mm, b)
                nc.vector.tensor_tensor(v_sb[:, :, :], v_ps,
                                        b2v_row[:, :].unsqueeze(1).to_broadcast([P, NT, C]), ALU.add
                                        ).then_inc(v_ready, 1)

            def mask_scores(b, n):
                dve.wait_ge(s_mm, n)
                freed(dve, a_mm, b)
                nc.vector.tensor_tensor(sT[:, :], s_ps, mask[:, :], ALU.mult).then_inc(s_ready, 1)

            def a_sums(b, n):
                dve.wait_ge(a_mm, n)
                for t in range(NT):
                    last = nc.vector.bn_stats(a_bst[:, t], a_ps[:, t])
                last.then_inc(a_stats, 1)

            def a_centre(b, n):
                own_instruction(dve)
                dve.wait_ge(a_stats, n)
                freed(dve, a_rstd, b)
                for t in range(NT):
                    last = nc.vector.bn_aggr(a_mv[:, t], a_bst[:, t])
                last.then_inc(a_moments, 1)
                dve.wait_ge(a_moments, n)
                nc.vector.tensor_scalar(a_ve[:, :], a_mv[:, :, 1], LN_EPS, None, ALU.add).then_inc(a_eps, 1)
                freed(dve, x1_ready, b)
                for t in range(NT):
                    last = nc.vector.scalar_tensor_tensor(out=ac[:, t], in0=a_ps[:, t], scalar=a_mv[:, t, 0:1],
                                                          in1=lnw_row[:, :], op0=ALU.subtract, op1=ALU.mult)
                last.then_inc(ac_ready, 1)

            def residual(b, n):
                dve.wait_ge(a_rstd, n)
                dve.wait_ge(ac_ready, n)
                dve.wait_ge(xb_ready, n)
                freed(dve, z_ready, b)
                freed(dve, x1_saved, 16 * b)
                for t in range(NT):
                    last = nc.vector.scalar_tensor_tensor(out=x1_cur[:, t], in0=ac[:, t], scalar=a_rs[:, t:t + 1],
                                                          in1=xb[:, t], op0=ALU.mult, op1=ALU.add)
                last.then_inc(x1_ready, 1)

            def z_sums(b, n):
                dve.wait_ge(x1_ready, n)
                for t in range(NT):
                    last = nc.vector.bn_stats(z_bst[:, t], x1_cur[:, t])
                last.then_inc(z_stats, 1)

            def z_variance(b, n):
                own_instruction(dve)
                dve.wait_ge(z_stats, n)
                freed(dve, z_ready, b)
                for t in range(NT):
                    last = nc.vector.bn_aggr(z_mv[:, t], z_bst[:, t])
                last.then_inc(z_moments, 1)
                dve.wait_ge(z_moments, n)
                nc.vector.tensor_scalar(z_u[:, :], z_mv[:, :, 1], LN_EPS, RMS_EPS ** 2 / C, ALU.add, ALU.mult
                                        ).then_inc(z_u_set, 1)
                nc.vector.tensor_scalar(z_nm[:, :], z_mv[:, :, 0], -1.0, None, ALU.mult)
                dve.wait_ge(z_u_set, n)
                nc.vector.tensor_tensor(z_w[:, :], z_mv[:, :, 1], z_u[:, :], ALU.max).then_inc(z_w_set, 1)

            def zT_rest(b, n):
                dve.wait_ge(zT_hi, n)
                nc.vector.tensor_tensor(zT_all[:, b, LO], zT_ps, zT_all[:, b, HI].bitcast(F32), ALU.subtract
                                        ).then_inc(zT_lo, 1)

            def max_D(b, n):
                dve.wait_ge(LT_mm, n)
                freed(dve, D_exp, b)
                nc.vector.tensor_reduce(nmD[:, :], LT_ps, AX.X, ALU.max, negate=True).then_inc(D_max, 1)

            def max_C(b, n):
                dve.wait_ge(L_mm, n)
                freed(dve, C_exp, b)
                nc.vector.tensor_reduce(nmC[:, :], L_ps, AX.X, ALU.max, negate=True).then_inc(C_max, 1)

            def invert_ZD(h):
                def stage(b, n):
                    dve.wait_ge((D_exp_half, D_exp)[h], n)
                    freed(dve, Dn_ready, b)
                    nc.vector.reciprocal(rZD[:, 2 * h:2 * h + 2], ZD[:, 2 * h:2 * h + 2]).then_inc(ZD_inv[h], 1)
                return stage

            def D_rest(b, n):
                dve.wait_ge(D_hi, n)
                nc.vector.tensor_tensor(D_sb[:, LO], D_ps, D_sb[:, HI].bitcast(F32), ALU.subtract).then_inc(D_lo, 1)

            def CT_copy0(b, n):
                dve.wait_ge(C_turned[0], n)
                nc.vector.tensor_copy(CT_all[:, b, 0:2], CT_ps(b, 0)).then_inc(CT_ready[0], 1)
                nc.vector.reciprocal(rZC_all[:, b], ZC_all[:, b]).then_inc(ZC_inv, 1)

            def slots_rest(b, n):
                dve.wait_ge(slots_hi, n)
                nc.vector.scalar_tensor_tensor(out=slots_all[:, b, LO], in0=slots_ps, scalar=gx_col[:, 0:1],
                                               in1=slots_all[:, b, HI].bitcast(F32), op0=ALU.mult,
                                               op1=ALU.subtract).then_inc(slots_lo, 1)

            def h_rest(g):
                def stage(b, n):
                    dve.wait_ge(h_hi_ready, NG * b + g + 1)
                    freed(dve, PT_mm, NG * b + g - 1)
                    nc.vector.tensor_tensor(h_lo[:, g], h_f[:, g], h_hi[:, g].bitcast(F32), ALU.subtract
                                            ).then_inc(h_lo_ready, 1)
                return stage

            def PT_copy(b, n):
                dve.wait_ge(PT_mm, NG * b + NG)
                freed(dve, P_turned, b)
                nc.vector.tensor_copy(PT_sb[:, :], PT_ps).then_inc(PT_ready, 1)

            def finish(b, n):
                dve.wait_ge(out_mm, n)
                dve.wait_ge(ZC_inv, n)
                dve.wait_ge(x1_saved, 16 * n)
                freed(dve, out_stored, 16 * b)
                for t in range(NT):
                    last = nc.vector.scalar_tensor_tensor(out=out_sb[:, t], in0=out_ps[:, t],
                                                          scalar=rZC_all[:, b, t:t + 1], in1=x1_all[:, b, t],
                                                          op0=ALU.mult, op1=ALU.add)
                last.then_inc(out_ready, 1)

            def before_start():
                x_moments_of(0)
                x_bias(0)
                x_moments_of(1)

            def before_0():
                x_bias(1)
                x_moments_of(2)
                dve.wait_ge(ld_rows, 48)

            def before_2():
                x_bias(2)
                x_moments_of(3)
                slot_mean_square()

            run(dve, [[(-1, mask_scores), (-2, residual), (-2, z_sums), (-2, z_variance), (-1, a_sums), (-3, zT_rest),
                       (-1, a_centre), (0, v_bias)],
                      [(LATE - 1, mask_scores), (LATE - 2, residual), (LATE - 2, z_sums), (LATE - 2, z_variance),
                       (1, max_D), (LATE - 1, a_sums), (LATE - 3, zT_rest), (LATE - 1, a_centre),
                       (0, D_rest), (1, invert_ZD(0)), (1, max_C), (1, invert_ZD(1)), (0, CT_copy0), (0, slots_rest)],
                      [(1, max_D), (0, D_rest), (1, invert_ZD(0)), (1, max_C), (1, invert_ZD(1)), (0, CT_copy0),
                       (0, slots_rest)],
                      [(0, D_rest), (FIRST, h_rest(0)), (0, slots_rest), (0, CT_copy0), (FIRST, h_rest(1))],
                      [(0, PT_copy), (1, h_rest(0)), (1, h_rest(1)), (-1, finish)]],
                {(ATTN, -1): before_start, (ATTN, 0): before_0,
                 (ATTN, 1): lambda: dve.wait_ge(mask_set, 3), (ATTN, 2): before_2,
                 (ATTN, 3): lambda: x_bias(3), (ATTN, 4): slot_normalise,
                 (ATTN, B - 1): slot_rest})

        @block.tensor
        def _(pe):
            def three_pass(dst, stationary, moving, start, stop):
                nc.tensor.matmul(dst, stationary(HI), moving(HI), start=start, stop=False)
                nc.tensor.matmul(dst, stationary(HI), moving(LO), start=False, stop=False)
                return nc.tensor.matmul(dst, stationary(LO), moving(HI), start=False, stop=stop)

            def turn_x(b, n):
                pe.wait_ge(xn_ready, n)
                freed(pe, xT_ready, b)
                for t in range(NT):
                    last = nc.tensor.transpose(xT_ps[:, t * P:(t + 1) * P], xn[:, t], ident[:, :])
                last.then_inc(x_turned, 1)

            def hidden_qk(b, n):
                pe.wait_ge(xT_ready, n)
                freed(pe, hid_ready, 3 * b)
                for m in range(2):
                    last = nc.tensor.matmul(hqk_ps[:, m], W1_sb[:, m], xT[:, :], start=True, stop=True)
                last.then_inc(hid_mm, 1)

            def hidden_v(b, n):
                nc.tensor.matmul(hv_ps, W1_sb[:, 2], xT[:, :], start=True, stop=True).then_inc(hid_mm, 1)

            def project(b, n):
                if first_batch(b):
                    pe.wait_ge(ld_W2, 48)
                freed(pe, qk_ready, 2 * b)
                for m in range(2):
                    pe.wait_ge(hid_ready, 3 * b + m + 1)
                    last = nc.tensor.matmul(qk_ps[:, m], W2_sb[:, m], hidT[:, m], start=True, stop=True)
                last.then_inc(qk_mm, 1)
                pe.wait_ge(hid_ready, 3 * b + 3)
                freed(pe, v_ready, b)
                for t in range(NT):
                    last = nc.tensor.matmul(v_ps[:, t], hidT[:, 2, t * P:(t + 1) * P], W2_sb[:, 2],
                                            start=True, stop=True)
                last.then_inc(v_mm, 1)

            def scores(b, n):
                pe.wait_ge(qk_ready, 2 * b + 2)
                freed(pe, s_ready, b)
                nc.tensor.matmul(s_ps[:, 0:T], qkT[:, 1, 0:P], qkT[:, 0], start=True, stop=True)
                nc.tensor.matmul(s_ps[:, T:SW], qkT[:, 1, P:T], qkT[:, 0, P:T], start=True, stop=True
                                 ).then_inc(s_mm, 1)

            def attend(b, n):
                pe.wait_ge(s_ready, n)
                pe.wait_ge(v_ready, n)
                freed(pe, ac_ready, b)
                nc.tensor.matmul(a_ps[:, 0], sT[:, 0:P], v_sb[:, 0], start=True, stop=True)
                nc.tensor.matmul(a_ps[:, 1], sT[:, P:T], v_sb[:, 0], start=True, stop=False)
                nc.tensor.matmul(a_ps[:, 1], sT[:, T:SW], v_sb[:, 1], start=False, stop=True).then_inc(a_mm, 1)

            def turn_z(b, n):
                pe.wait_ge(z_ready, n)
                freed(pe, zT_hi, b)
                freed(pe, zT_lo, b)
                for t in range(NT):
                    last = nc.tensor.transpose(zT_ps[:, t * P:(t + 1) * P], z_cur[:, t], ident[:, :])
                last.then_inc(z_turned, 1)

            def turn_slots():
                pe.wait_ge(slot_n_set, 1)
                pe.wait_ge(xT_ready, B)
                for e in range(NE):
                    last = nc.tensor.transpose(slotT_ps[:, e * P:(e + 1) * P], slot_n[:, e], ident[:, :])
                last.then_inc(slot_turned, 1)

            def logits_T(b, n):
                pe.wait_ge(zT_hi, n)
                pe.wait_ge(zT_lo, n)
                freed(pe, D_exp, b)
                if first_batch(b):
                    pe.wait_ge(slotT_lo, 1)
                    pe.wait_ge(hid_ready, 3 * B)
                    pe.wait_ge(qk_ready, 2 * B)
                    pe.wait_ge(v_ready, B)
                for e in range(NE):
                    last = three_pass(LT_ps[:, e], lambda s: slotT_s[:, s, e * P:(e + 1) * P],
                                      lambda s: zT_all[:, b, s], True, True)
                last.then_inc(LT_mm, 1)

            def logits(b, n):
                pe.wait_ge(zT_staged, 16 * n)
                freed(pe, C_exp, b)
                for t in range(NT):
                    last = three_pass(L_ps[:, t], lambda s: zT_st[:, s, t * P:(t + 1) * P],
                                      lambda s: slotT_s[:, s], True, True)
                last.then_inc(L_mm, 1)

            def turn_D(b, n):
                pe.wait_ge(Dn_ready, n)
                freed(pe, CT_ready[0], b)
                if isinstance(b, int) and b == 1:
                    pe.wait_ge(CT_ready[1], 1)
                if first_batch(b):
                    pe.wait_ge(s_ready, B)
                    pe.wait_ge(ac_ready, B)
                for t in range(NT):
                    for e in range(NE):
                        last = nc.tensor.transpose(D_ps[:, t, e * P:(e + 1) * P], Dn[:, e, t * P:(t + 1) * P],
                                                   ident[:, :])
                last.then_inc(D_turned, 1)

            def turn_C(h):
                def stage(b, n):
                    pe.wait_ge(C_exp, n)
                    if h == 0 or first_batch(b):
                        pe.wait_ge(D_lo, n)
                    elif isinstance(b, int) and b == 1:
                        pe.wait_ge(zT_lo, B)
                    else:
                        pe.wait_ge(CT_ready[1], b)
                    for e in range(2 * h, 2 * h + 2):
                        for t in range(NT):
                            last = nc.tensor.transpose(CT_ps(b, h)[:, e - 2 * h, t * P:(t + 1) * P],
                                                       Cx[:, t, e * P:(e + 1) * P], ident[:, :])
                    last.then_inc(C_turned[h], 1)
                return stage

            def slots_with_D_hi(b, n):
                pe.wait_ge(z_lo, n)
                pe.wait_ge(D_hi, n)
                freed(pe, slots_lo, b)
                for t in range(NT):
                    for z_part in (HI, LO):
                        nc.tensor.matmul(slots_ps, z_st[:, z_part, t], D_sb[:, HI, t],
                                         start=(t == 0 and z_part == HI), stop=False)

            def slots_with_D_lo(b, n):
                pe.wait_ge(D_lo, n)
                for t in range(NT):
                    last = nc.tensor.matmul(slots_ps, z_st[:, HI, t], D_sb[:, LO, t], start=False, stop=(t == NT - 1))
                last.then_inc(slots_mm, 1)

            def expert_hidden(g):
                def stage(b, n):
                    pe.wait_ge(slots_hi, n)
                    pe.wait_ge(slots_lo, n)
                    freed(pe, h_ready, NG * b + g - 1)
                    if first_batch(b):
                        pe.wait_ge(w_lo, 2)
                        pe.wait_ge((D_exp, C_exp)[g], B)
                    for j in range(GH):
                        m = g * GH + j
                        last = three_pass(h_ps[g][:, j], lambda s: w1_s[:, s, m * P:(m + 1) * P],
                                          lambda s: slots_all[:, b, s], True, True)
                    last.then_inc(h_mm, 1)
                return stage

            def expert_out(g):
                def stage(b, n):
                    pe.wait_ge(h_hi_ready, NG * b + g + 1)
                    pe.wait_ge(h_lo_ready, NG * b + g + 1)
                    if g == 0:
                        freed(pe, PT_ready, b)
                        if first_batch(b):
                            pe.wait_ge(D_lo, B)
                    for j in range(GH):
                        m = g * GH + j
                        last = three_pass(PT_ps, lambda s: w2_s[:, s, m],
                                          lambda s: (h_hi, h_lo)[s][:, g, j], m == 0, m == NH - 1)
                    last.then_inc(PT_mm, 1)
                return stage

            def turn_P(b, n):
                pe.wait_ge(PT_ready, n)
                freed(pe, P_ready, b)
                if first_batch(b):
                    pe.wait_ge(CT_ready[0], B)
                    pe.wait_ge(CT_ready[1], B)
                for e in range(NE):
                    last = nc.tensor.transpose(P_ps[:, e], PT_sb[:, e * P:(e + 1) * P], ident[:, :])
                last.then_inc(P_turned, 1)

            def combine(b, n):
                pe.wait_ge(P_ready, n)
                CT = CT_st
                if last_batch(b):
                    CT = CT_all[:, b]
                else:
                    pe.wait_ge(CT_staged, 16 * n)
                freed(pe, out_ready, b)
                for t in range(NT):
                    for e in range(NE):
                        last = nc.tensor.matmul(out_ps[:, t], CT[:, e, t * P:(t + 1) * P], P_sb[:, e],
                                                start=(e == 0), stop=(e == NE - 1))
                last.then_inc(out_mm, 1)

            def weights_in():
                pe.wait_ge(ld_W1, 48)

            run(pe, [[(0, hidden_qk), (-1, scores), (0, hidden_v), (-3, turn_z), (1, turn_x), (-1, attend), (0, project)],
                     [(LATE - 1, scores), (LATE - 3, turn_z), (1, logits_T), (LATE - 1, attend), (0, turn_D),
                      (1, logits), (0, slots_with_D_hi), (0, turn_C(1)),
                      (0, slots_with_D_lo), (0, turn_C(0))],
                     [(1, logits_T), (0, turn_D), (1, logits), (0, slots_with_D_hi), (0, turn_C(1)),
                      (0, slots_with_D_lo), (0, turn_C(0))],
                     [(FIRST, expert_hidden(0)), (0, turn_D), (FIRST, expert_hidden(1)), (0, slots_with_D_hi), (0, turn_C(1)),
                      (0, slots_with_D_lo), (0, turn_C(0))],
                     [(1, expert_hidden(0)), (0, expert_out(0)), (1, expert_hidden(1)), (0, expert_out(1)),
                      (-1, combine), (0, turn_P)]],
                {(ATTN, -1): lambda: pe.wait_ge(ident_set, 2), (ATTN, 0): weights_in,
                 (ATTN, B - 1): turn_slots})


_INS = ['L0_attn_x', 'L0_attn_W1q', 'L0_attn_b1q', 'L0_attn_W2q', 'L0_attn_b2q', 'L0_attn_W1k', 'L0_attn_b1k',
        'L0_attn_W2k', 'L0_attn_b2k', 'L0_attn_W1v', 'L0_attn_b1v', 'L0_attn_W2v', 'L0_attn_b2v', 'L0_attn_ln_w',
        'L0_attn_ln_b', 'L0_ffn_gamma_x', 'L0_ffn_gamma_slot', 'L0_ffn_slot_embeds', 'L0_ffn_w1', 'L0_ffn_w2']
_OUTS = [((8, 256, 128), 'float32')]


def kernel(**inputs):
    import numpy as _np
    import concourse.bacc as _bacc
    from concourse import mybir as _mybir
    from concourse.bass_utils import run_bass_kernel_spmd as _run

    nc = _bacc.Bacc("TRN2", target_bir_lowering=False, num_devices=1)
    arrays, args = {}, []
    for name in _INS:
        a = _np.ascontiguousarray(inputs[name])
        arrays[f"in_{name}_dram"] = a
        args.append(nc.dram_tensor(f"in_{name}_dram", a.shape, _mybir.dt.from_np(a.dtype), kind="ExternalInput").ap())
    for i, (shape, dtype) in enumerate(_OUTS):
        dt = _mybir.dt.from_np(_np.dtype(dtype))
        args.append(nc.dram_tensor(f"out_{i}_dram", shape, dt, kind="ExternalOutput").ap())
    build(nc, *args)
    r = _run(nc, [arrays], core_ids=[0])
    got = tuple(r.results[0][f"out_{i}_dram"] for i in range(len(_OUTS)))
    return got[0]
```
